# Optimizing a Trainium2 kernel written in Bass

```python
import numpy as np
import jax
import jax.numpy as jnp

def _softmax(x, axis=-1):
    return jax.nn.softmax(x, axis=axis)
def _gelu(x):
    return jax.nn.gelu(x, approximate=True)
def _silu(x):
    return jax.nn.silu(x)
def _sigmoid(x):
    return jax.nn.sigmoid(x)
def _layernorm(x, axis=-1, eps=1e-5):
    m = jnp.mean(x, axis=axis, keepdims=True)
    v = jnp.var(x, axis=axis, keepdims=True)
    return (x - m) / jnp.sqrt(v + eps)
def _scatter_add(tgt, idx, src, axis=0):
    return tgt.at[idx].add(src)
def _segment_sum(src, seg, n):
    return jax.ops.segment_sum(src, seg, n)

kernel_name = 'mk_conv_seq_d2_conv_nhwc128_96ce93'

def setup_inputs(seed: int = 0):
    np.random.seed(seed)
    _w = jnp.asarray
    def _rec_inputs():
        import jax
        import jax.numpy as jnp
        _gk = jax.random.key(seed)
        x = 7.22e-05 + 1 * jax.random.normal(jax.random.fold_in(_gk, 1), (1, 256, 256, 128), jnp.float32)
        return x
    x = _rec_inputs()
    def _L0_conv_setup():
        import jax, jax.numpy as jnp
        import numpy as np
        DIM = 128
        N_HEADS = 4
        HEAD_DIM = DIM // N_HEADS
        EPS = 1e-05
        key = jax.random.key(seed)
        ks = jax.random.split(key, 6)
        B, L, D = (1, 256, DIM)
        s = 1.0 / np.sqrt(D)
        return {'z': jax.random.normal(ks[0], (B, L, L, D), dtype=jnp.float32), 'ln_g': jnp.ones((D,), dtype=jnp.float32), 'ln_b': jnp.zeros((D,), dtype=jnp.float32), 'w_qkv': jax.random.normal(ks[1], (D, 3 * D), dtype=jnp.float32) * s, 'b_qkv': jnp.zeros((3 * D,), dtype=jnp.float32), 'w_proj': jax.random.normal(ks[2], (D, D), dtype=jnp.float32) * s, 'b_proj': jnp.zeros((D,), dtype=jnp.float32)}
    _L0_conv_all = _L0_conv_setup()
    _L0_conv_in = {k: v for k, v in _L0_conv_all.items() if k in ('ln_g', 'ln_b', 'w_qkv', 'b_qkv', 'w_proj', 'b_proj', )}
    del _L0_conv_all

    def _L1_conv_setup():
        import jax, jax.numpy as jnp
        import numpy as np
        EPS = 1e-05
        N = 384
        CZ = 128
        CH = 128

        def _layer_norm(x, w, b):
            m = jnp.mean(x, axis=-1, keepdims=True)
            v = jnp.mean(jnp.square(x - m), axis=-1, keepdims=True)
            return (x - m) * jax.lax.rsqrt(v + EPS) * w + b

        def _tri_mul(z, outgoing, ln_in_w, ln_in_b, w_ag, b_ag, w_ap, b_ap, w_bg, b_bg, w_bp, b_bp, ln_out_w, ln_out_b, w_z, b_z, w_g, b_g):
            zn = _layer_norm(z, ln_in_w, ln_in_b)
            a = jax.nn.sigmoid(zn @ w_ag + b_ag) * (zn @ w_ap + b_ap)
            b = jax.nn.sigmoid(zn @ w_bg + b_bg) * (zn @ w_bp + b_bp)
            if outgoing:
                p = jnp.einsum('bijc,bkjc->bikc', a, b)
            else:
                p = jnp.einsum('bjic,bjkc->bikc', a, b)
            p = _layer_norm(p, ln_out_w, ln_out_b) @ w_z + b_z
            g = jax.nn.sigmoid(zn @ w_g + b_g)
            return p * g
        key = jax.random.key(seed)
        ks = jax.random.split(key, 8)
        s = 0.02
        return {'z': jax.random.normal(ks[0], (1, N, N, CZ), jnp.float32), 'ln_in_w': jnp.ones((2, CZ), jnp.float32), 'ln_in_b': jnp.zeros((2, CZ), jnp.float32), 'w_ag': jax.random.normal(ks[1], (2, CZ, CH), jnp.float32) * s, 'b_ag': jnp.zeros((2, CH), jnp.float32), 'w_ap': jax.random.normal(ks[2], (2, CZ, CH), jnp.float32) * s, 'b_ap': jnp.zeros((2, CH), jnp.float32), 'w_bg': jax.random.normal(ks[3], (2, CZ, CH), jnp.float32) * s, 'b_bg': jnp.zeros((2, CH), jnp.float32), 'w_bp': jax.random.normal(ks[4], (2, CZ, CH), jnp.float32) * s, 'b_bp': jnp.zeros((2, CH), jnp.float32), 'ln_out_w': jnp.ones((2, CH), jnp.float32), 'ln_out_b': jnp.zeros((2, CH), jnp.float32), 'w_z': jax.random.normal(ks[5], (2, CH, CZ), jnp.float32) * s, 'b_z': jnp.zeros((2, CZ), jnp.float32), 'w_g': jax.random.normal(ks[6], (2, CZ, CZ), jnp.float32) * s, 'b_g': jnp.zeros((2, CZ), jnp.float32)}
    _L1_conv_all = _L1_conv_setup()
    _L1_conv_in = {k: v for k, v in _L1_conv_all.items() if k in ('ln_in_w', 'ln_in_b', 'w_ag', 'b_ag', 'w_ap', 'b_ap', 'w_bg', 'b_bg', 'w_bp', 'b_bp', 'ln_out_w', 'ln_out_b', 'w_z', 'b_z', 'w_g', 'b_g', )}
    del _L1_conv_all

    return {
        "x": x,
        "L0_conv_ln_g": _L0_conv_in["ln_g"],
        "L0_conv_ln_b": _L0_conv_in["ln_b"],
        "L0_conv_w_qkv": _L0_conv_in["w_qkv"],
        "L0_conv_b_qkv": _L0_conv_in["b_qkv"],
        "L0_conv_w_proj": _L0_conv_in["w_proj"],
        "L0_conv_b_proj": _L0_conv_in["b_proj"],
        "L1_conv_ln_in_w": _L1_conv_in["ln_in_w"],
        "L1_conv_ln_in_b": _L1_conv_in["ln_in_b"],
        "L1_conv_w_ag": _L1_conv_in["w_ag"],
        "L1_conv_b_ag": _L1_conv_in["b_ag"],
        "L1_conv_w_ap": _L1_conv_in["w_ap"],
        "L1_conv_b_ap": _L1_conv_in["b_ap"],
        "L1_conv_w_bg": _L1_conv_in["w_bg"],
        "L1_conv_b_bg": _L1_conv_in["b_bg"],
        "L1_conv_w_bp": _L1_conv_in["w_bp"],
        "L1_conv_b_bp": _L1_conv_in["b_bp"],
        "L1_conv_ln_out_w": _L1_conv_in["ln_out_w"],
        "L1_conv_ln_out_b": _L1_conv_in["ln_out_b"],
        "L1_conv_w_z": _L1_conv_in["w_z"],
        "L1_conv_b_z": _L1_conv_in["b_z"],
        "L1_conv_w_g": _L1_conv_in["w_g"],
        "L1_conv_b_g": _L1_conv_in["b_g"],
    }

def reference(x, L0_conv_ln_g, L0_conv_ln_b, L0_conv_w_qkv, L0_conv_b_qkv, L0_conv_w_proj, L0_conv_b_proj, L1_conv_ln_in_w, L1_conv_ln_in_b, L1_conv_w_ag, L1_conv_b_ag, L1_conv_w_ap, L1_conv_b_ap, L1_conv_w_bg, L1_conv_b_bg, L1_conv_w_bp, L1_conv_b_bp, L1_conv_ln_out_w, L1_conv_ln_out_b, L1_conv_w_z, L1_conv_b_z, L1_conv_w_g, L1_conv_b_g):
    import jax
    import jax.numpy as jnp
    def _L0_conv_ref(z, ln_g, ln_b, w_qkv, b_qkv, w_proj, b_proj):
        import jax, jax.numpy as jnp
        import numpy as np
        DIM = 128
        N_HEADS = 4
        HEAD_DIM = DIM // N_HEADS
        EPS = 1e-05
        B, L1, L2, D = z.shape
        H, hd = (N_HEADS, HEAD_DIM)
        mu = jnp.mean(z, axis=-1, keepdims=True)
        var = jnp.mean(jnp.square(z - mu), axis=-1, keepdims=True)
        zn = (z - mu) * jax.lax.rsqrt(var + EPS) * ln_g + ln_b
        qkv = zn @ w_qkv + b_qkv
        qkv = qkv.reshape(B, L1, L2, 3, H, hd)
        q, k, v = (qkv[..., 0, :, :], qkv[..., 1, :, :], qkv[..., 2, :, :])
        scale = 1.0 / jnp.sqrt(jnp.asarray(hd, dtype=z.dtype))
        attn = jnp.einsum('brqhd,brkhd->brhqk', q, k) * scale
        attn = jax.nn.softmax(attn, axis=-1)
        out = jnp.einsum('brhqk,brkhd->brqhd', attn, v)
        out = out.reshape(B, L1, L2, D)
        out = out @ w_proj + b_proj
        return z + out

    def _L1_conv_ref(z, ln_in_w, ln_in_b, w_ag, b_ag, w_ap, b_ap, w_bg, b_bg, w_bp, b_bp, ln_out_w, ln_out_b, w_z, b_z, w_g, b_g):
        import jax, jax.numpy as jnp
        import numpy as np
        EPS = 1e-05
        N = 384
        CZ = 128
        CH = 128

        def _layer_norm(x, w, b):
            m = jnp.mean(x, axis=-1, keepdims=True)
            v = jnp.mean(jnp.square(x - m), axis=-1, keepdims=True)
            return (x - m) * jax.lax.rsqrt(v + EPS) * w + b

        def _tri_mul(z, outgoing, ln_in_w, ln_in_b, w_ag, b_ag, w_ap, b_ap, w_bg, b_bg, w_bp, b_bp, ln_out_w, ln_out_b, w_z, b_z, w_g, b_g):
            zn = _layer_norm(z, ln_in_w, ln_in_b)
            a = jax.nn.sigmoid(zn @ w_ag + b_ag) * (zn @ w_ap + b_ap)
            b = jax.nn.sigmoid(zn @ w_bg + b_bg) * (zn @ w_bp + b_bp)
            if outgoing:
                p = jnp.einsum('bijc,bkjc->bikc', a, b)
            else:
                p = jnp.einsum('bjic,bjkc->bikc', a, b)
            p = _layer_norm(p, ln_out_w, ln_out_b) @ w_z + b_z
            g = jax.nn.sigmoid(zn @ w_g + b_g)
            return p * g
        for idx, outgoing in enumerate((True, False)):
            z = z + _tri_mul(z, outgoing, ln_in_w[idx], ln_in_b[idx], w_ag[idx], b_ag[idx], w_ap[idx], b_ap[idx], w_bg[idx], b_bg[idx], w_bp[idx], b_bp[idx], ln_out_w[idx], ln_out_b[idx], w_z[idx], b_z[idx], w_g[idx], b_g[idx])
        return z

    def _gn(v, G=32, eps=1e-5):
        B_, H_, W_, C_ = v.shape
        g = v.reshape(B_, H_, W_, G, C_ // G)
        m = jnp.mean(g, axis=(1, 2, 4), keepdims=True)
        s = jnp.var(g, axis=(1, 2, 4), keepdims=True)
        return ((g - m) / jnp.sqrt(s + eps)).reshape(v.shape)

    def _ln_c(v, eps=1e-6):
        m = jnp.mean(v, axis=-1, keepdims=True)
        s = jnp.var(v, axis=-1, keepdims=True)
        return (v - m) / jnp.sqrt(s + eps)

    def _ln_t(v, eps=1e-5):
        m = jnp.mean(v, axis=-1, keepdims=True)
        s = jnp.var(v, axis=-1, keepdims=True)
        return (v - m) / jnp.sqrt(s + eps)

    def _to_tokens(v):
        B_, H_, W_, C_ = v.shape
        return v.reshape(B_, H_ * W_, C_)
    def _from_tokens(t, like):
        return t.reshape(like.shape)

    x = _L0_conv_ref(x, L0_conv_ln_g, L0_conv_ln_b, L0_conv_w_qkv, L0_conv_b_qkv, L0_conv_w_proj, L0_conv_b_proj)
    x = _L1_conv_ref(x, L1_conv_ln_in_w, L1_conv_ln_in_b, L1_conv_w_ag, L1_conv_b_ag, L1_conv_w_ap, L1_conv_b_ap, L1_conv_w_bg, L1_conv_b_bg, L1_conv_w_bp, L1_conv_b_bp, L1_conv_ln_out_w, L1_conv_ln_out_b, L1_conv_w_z, L1_conv_b_z, L1_conv_w_g, L1_conv_b_g)
    return x


_drawn_inputs = setup_inputs


def setup_inputs(seed=0):
    import zlib

    import numpy as np

    out = dict(_drawn_inputs(seed))
    spreads = {'L0_conv_ln_g': (1.0, 0.2),
     'L0_conv_ln_b': (0.0, 0.1),
     'L0_conv_b_qkv': (0.0, 0.1),
     'L0_conv_b_proj': (0.0, 0.1),
     'L1_conv_ln_in_w': (1.0, 0.6),
     'L1_conv_ln_in_b': (0.0, 0.1),
     'L1_conv_b_ag': (0.0, 0.8),
     'L1_conv_b_ap': (0.0, 0.1),
     'L1_conv_b_bg': (0.0, 0.8),
     'L1_conv_b_bp': (0.0, 0.1),
     'L1_conv_ln_out_w': (1.0, 0.2),
     'L1_conv_ln_out_b': (0.0, 0.5),
     'L1_conv_b_z': (0.0, 0.1),
     'L1_conv_b_g': (0.0, 0.8)}
    factors = {'L1_conv_w_ag': 7.476, 'L1_conv_w_bg': 7.299}
    for name, (base, spread) in spreads.items():
        noise = np.random.default_rng([zlib.crc32(name.encode()), seed]).standard_normal(out[name].shape)
        drawn = base * np.exp(spread * noise) if base else spread * noise
        out[name] = jnp.asarray(drawn.astype(out[name].dtype))
    for name, factor in factors.items():
        out[name] = (out[name] * factor).astype(out[name].dtype)
    return out
```

```python
import math
from contextlib import ExitStack

import concourse.bass as bass
from concourse import mybir

P = 128
EPS = 1e-5

ALU = mybir.AluOpType
ACT = mybir.ActivationFunctionType
F32 = mybir.dt.float32
F32R = mybir.dt.float32r
BF16 = mybir.dt.bfloat16
AX_X = mybir.AxisListType.X




def attention_layer(nc, x, x_out, ln_g, ln_b, w_qkv, b_qkv, w_proj, b_proj):
    L, T, D = x.shape
    H, HD = 4, D // 4
    QT = T // P
    UNITS = QT * H // 2
    SCALE = 1.0 / math.sqrt(HD)
    assert D == P and QT == 2 and L % 2 == 0

    x_v = x.rearrange("r (p t) c -> r p t c", t=QT)
    out_v = x_out.rearrange("r (p t) c -> r p t c", t=QT)

    with ExitStack() as ctx:
        def sb(name, shape, dt=F32):
            return ctx.enter_context(nc.sbuf_tensor("at_" + name, shape, dt))

        def bank(name):
            return ctx.enter_context(nc.psum_tensor("at_" + name, [P, 512], F32))

        def sem(name):
            return ctx.enter_context(nc.semaphore("at_" + name))

        ident = sb("ident", [P, P])
        ident_bf = sb("ident_bf", [P, P], BF16)
        head_rows = sb("head_rows", [P, H, P], BF16)
        half_neg = sb("half_neg", [P, QT])
        eps = sb("eps", [P, QT])
        g_col, b_col = sb("g_col", [P, 1]), sb("b_col", [P, 1])
        w_raw, w = sb("w_raw", [P, 3 * D]), sb("w", [P, 3 * D])
        qkv_bias_raw = sb("qkv_bias_raw", [P, 3])
        qkv_bias = sb("qkv_bias", [P, 3])
        v_bias_wide = sb("v_bias_wide", [P, P])
        wp = sb("wp", [P, D])
        proj_bias_raw, proj_bias = sb("proj_bias_raw", [P, D]), sb("proj_bias", [P, D])
        x_in = [sb(f"x_in{i}", [P, QT, D]) for i in range(2)]
        stats = [sb(f"stats{i}", [P, QT, 6]) for i in range(2)]
        mean_var = [sb(f"mean_var{i}", [P, QT, 2]) for i in range(2)]
        var_eps = [sb(f"var_eps{i}", [P, QT]) for i in range(2)]
        rstd = [sb(f"rstd{i}", [P, QT]) for i in range(2)]
        xn = [sb(f"xn{i}", [P, QT, D]) for i in range(2)]
        k_hi, k_lo = ([sb(f"{n}{i}", [P, T], F32R) for i in range(2)] for n in ("k_hi", "k_lo"))
        q_hi, q_lo = ([sb(f"{n}{i}", [P, H, T], F32R) for i in range(2)] for n in ("q_hi", "q_lo"))
        v_one = [sb(f"v_one{i}", [P, QT, H, HD + 1]) for i in range(2)]
        row_max = [sb(f"row_max{i}", [P, QT, H]) for i in range(2)]
        max_hl = [sb(f"max_hl{i}", [P, QT, H, HD], BF16) for i in range(2)]
        x_res = [sb(f"x_res{i}", [P, QT, D]) for i in range(2)]
        x_bias = [sb(f"x_bias{i}", [P, QT, D]) for i in range(2)]
        y = [sb(f"y{i}", [P, QT, D]) for i in range(2)]
        zT = sb("zT", [P, T])
        neg_max = sb("neg_max", [P, T], BF16)
        pT = [sb(f"pT{i}", [P, QT, 2, T]) for i in range(2)]
        recip = sb("recip", [P, QT, H])
        att = sb("att", [P, QT, H, HD])
        attT = sb("attT", [P, T])

        bank_T, bank_qk, bank_v, bank_s = bank("bank_T"), bank("bank_qk"), bank("bank_v"), bank("bank_s")
        bank_sT = [bank(f"bank_sT{i}") for i in range(2)]
        banks_o = ctx.enter_context(nc.psum_tensor("at_banks_o", [P, QT, 512], F32))
        WIDE = H - 1
        FIRST_HEAD = [h // 2 for h in range(H)]
        O_COLS = WIDE * (HD + 1)
        O_OWN = [h * O_COLS + (h - FIRST_HEAD[h]) * (HD + 1) for h in range(H)]

        def own_sums(pair):
            step = O_OWN[2 * pair + 1] - O_OWN[2 * pair]
            return banks_o[:, :, O_OWN[2 * pair]:O_OWN[2 * pair] + 2 * step].rearrange("p t (h d) -> p t h d", h=2)

        w_loaded, consts_set, folded, folded_mm, folded_b = (sem(n) for n in ("w_loaded", "consts_set", "folded", "folded_mm", "folded_b"))
        x_loaded = [sem(f"x_loaded{i}") for i in range(2)]
        res_loaded = [sem(f"res_loaded{i}") for i in range(2)]
        y_stored = [sem(f"y_stored{i}") for i in range(2)]
        (stats_set, mean_set, eps_set, rstd_set, xn_set, zT_done, zT_copied, qk_done, hi_split, lo_split, v_done, v_copied,
         s_done, row_max_set, max_hi_set, max_split, maxT_done, neg_max_set, sT_done, p_set, pv_done, recip_set,
         att_set, attT_done, attT_copied, proj_done, x_bias_set, y_set) = (sem(n) for n in (
            "stats_set", "mean_set", "eps_set", "rstd_set", "xn_set", "zT_done", "zT_copied", "qk_done", "hi_split", "lo_split", "v_done",
            "v_copied", "s_done", "row_max_set", "max_hi_set", "max_split", "maxT_done", "neg_max_set", "sT_done", "p_set", "pv_done",
            "recip_set", "att_set", "attT_done", "attT_copied", "proj_done", "x_bias_set", "y_set"))

        class Slot:

            def __init__(self, it, s0):
                self.it, self.s0, self.loop = it, s0, not isinstance(it, int)

            def has(self, k):
                return self.loop or 0 <= self.s0 + k < L

            def row(self, k):
                return self.it * 2 + (self.s0 + k)

            def turn(self, k):
                return self.it + (self.s0 + k) // 2

            def buf(self, k):
                return (self.s0 + k) % 2

        FIRST, LOOP_FROM = -2, 4

        def all_slots(engine, slot):
            for s in range(FIRST, LOOP_FROM):
                slot(engine, Slot(0, s))
            n = (L - 2 - LOOP_FROM) // 2
            with engine.Fori(0, n) as it:
                for par in range(2):
                    slot(engine, Slot(it, LOOP_FROM + par))
            for s in range(LOOP_FROM + 2 * n, L + 2):
                slot(engine, Slot(0, s))

        def wait(engine, s, value):
            if not isinstance(value, int) or value > 0:
                engine.wait_ge(s, value)

        with nc.Block() as block:

            @block.sync
            def _(sp):
                sp.dma_start(g_col[:], ln_g.rearrange("(c a) -> c a", a=1)).then_inc(w_loaded, 16)
                sp.dma_start(b_col[:], ln_b.rearrange("(c a) -> c a", a=1)).then_inc(w_loaded, 16)
                sp.dma_start(w_raw[:], w_qkv).then_inc(w_loaded, 16)
                sp.dma_start(wp[:], w_proj).then_inc(w_loaded, 16)
                for i in range(3):
                    sp.dma_start(qkv_bias_raw[:, i:i + 1], b_qkv[i * D:(i + 1) * D].rearrange("(c a) -> c a", a=1)).then_inc(w_loaded, 16)
                sp.dma_start(proj_bias_raw[:], b_proj.rearrange("(a c) -> a c", a=1).to_broadcast([P, D])).then_inc(w_loaded, 16)

                def slot(sp, s):
                    if s.has(2):
                        wait(sp, xn_set, s.row(1))
                        sp.dma_start(x_in[s.buf(2)][:], x_v[s.row(2)]).then_inc(x_loaded[s.buf(2)], 16)
                    if s.has(-1):
                        wait(sp, x_bias_set, s.row(-2))
                        sp.dma_start(x_res[s.buf(-1)][:], x_v[s.row(-1)]).then_inc(res_loaded[s.buf(-1)], 16)
                    if s.has(-2):
                        sp.wait_ge(y_set, s.row(-1))
                        sp.dma_start(out_v[s.row(-2)], y[s.buf(-2)][:]).then_inc(y_stored[s.buf(-2)], 16)

                all_slots(sp, slot)
                for i in range(2):
                    sp.wait_ge(y_stored[i], 16 * (L // 2))

            @block.gpsimd
            def _(pool):
                nc.gpsimd.memset(ident[:], 0.0)
                nc.gpsimd.memset(half_neg[:], -0.5)
                nc.gpsimd.memset(eps[:], EPS)
                nc.gpsimd.memset(head_rows[:], 0.0)
                for i in range(2):
                    nc.gpsimd.memset(v_one[i][:], 1.0)
                    nc.gpsimd.memset(max_hl[i][:], 0.0)
                    nc.gpsimd.memset(q_hi[i][:].bitcast(F32), 0.0)
                    nc.gpsimd.memset(q_lo[i][:].bitcast(F32), 0.0)
                nc.gpsimd.memset(ident_bf[:], 0.0).then_inc(consts_set, 1)
                pool.wait_ge(consts_set, 1)
                for h in range(H):
                    nc.gpsimd.memset(head_rows[HD * h:HD * (h + 1), h, :], 1.0).then_inc(consts_set, 1)
                    pool.wait_ge(consts_set, h + 2)
                nc.gpsimd.affine_select(out=ident[:], in_=ident[:], compare_op=ALU.not_equal, fill=1.0, base=0,
                                        pattern=[[-1, P]], channel_multiplier=1)
                nc.gpsimd.affine_select(out=ident_bf[:], in_=ident_bf[:], compare_op=ALU.not_equal, fill=1.0, base=0,
                                        pattern=[[-1, P]], channel_multiplier=1).then_inc(consts_set, 1)

                def slot(pool, s):
                    if s.has(-2):
                        b = s.buf(-2)
                        if s.s0 + -2 == 0 and not s.loop:
                            pool.wait_ge(folded_b, 3)
                        pool.wait_ge(res_loaded[b], (s.turn(-2) + 1) * 16)
                        wait(pool, y_set, s.row(-3))
                        nc.gpsimd.tensor_tensor(x_bias[b][:], x_res[b][:], proj_bias[:].rearrange("p (a c) -> p a c", a=1).to_broadcast([P, QT, D]),
                                                ALU.add).then_inc(x_bias_set, 1)
                    if s.has(1):
                        b = s.buf(1)
                        pool.wait_ge(mean_set, s.row(2))
                        nc.gpsimd.tensor_tensor(var_eps[b][:], mean_var[b][:, :, 1], eps[:], ALU.add).then_inc(eps_set, 1)
                        pool.wait_ge(eps_set, s.row(2))
                        nc.gpsimd.tensor_tensor(rstd[b][:], var_eps[b][:], half_neg[:], ALU.pow).then_inc(rstd_set, 1)

                all_slots(pool, slot)

            @block.vector
            def _(dve):
                dve.wait_ge(w_loaded, 8 * 16)
                dve.wait_ge(consts_set, 1)
                nc.vector.tensor_scalar(w[:], w_raw[:], g_col[:, 0:1], None, ALU.mult).then_inc(folded, 1)
                dve.wait_ge(folded_mm, 1)
                nc.vector.tensor_tensor(qkv_bias[:], bank_T[:, 0:3], qkv_bias_raw[:], ALU.add).then_inc(folded_b, 1)
                dve.wait_ge(folded_b, 1)
                nc.vector.tensor_copy(v_bias_wide[:], qkv_bias[:, 2:3].to_broadcast([P, P])).then_inc(folded_b, 1)
                dve.wait_ge(folded_mm, 2)
                nc.vector.tensor_tensor(proj_bias[:], bank_T[:, 0:D], proj_bias_raw[:], ALU.add).then_inc(folded_b, 1)

                def slot(dve, s):
                    if s.has(-2):
                        dve.wait_ge(pv_done, s.row(-1) * H)
                        for pair in range(H // 2):
                            last = nc.vector.reciprocal(recip[:, :, 2 * pair:2 * pair + 2], own_sums(pair)[:, :, :, HD])
                        last.then_inc(recip_set, 1)
                        dve.wait_ge(recip_set, s.row(-1))
                        wait(dve, attT_done, s.row(-2))
                        for pair in range(H // 2):
                            last = nc.vector.tensor_tensor(att[:, :, 2 * pair:2 * pair + 2, :], own_sums(pair)[:, :, :, 0:HD],
                                                           recip[:, :, 2 * pair:2 * pair + 2].rearrange("p t (h d) -> p t h d", d=1).to_broadcast([P, QT, 2, HD]),
                                                           ALU.mult)
                        last.then_inc(att_set, 1)
                    if s.has(1):
                        b = s.buf(1)
                        dve.wait_ge(x_loaded[b], (s.turn(1) + 1) * 16)
                        wait(dve, rstd_set, s.row(0))
                        for t in range(QT):
                            last = nc.vector.bn_stats(stats[b][:, t, :], x_in[b][:, t, :])
                        last.then_inc(stats_set, 1)
                    if s.has(1):
                        dve.wait_ge(stats_set, s.row(2))
                    if s.has(-2):
                        b = s.buf(-2)
                        dve.wait_ge(proj_done, s.row(-1))
                        dve.wait_ge(x_bias_set, s.row(-1))
                        wait(dve, y_stored[b], s.turn(-2) * 16)
                        nc.vector.tensor_tensor(y[b][:], bank_v[:, 0:QT * D].rearrange("p (t c) -> p t c", t=QT), x_bias[b][:],
                                                ALU.add).then_inc(y_set, 1)
                    if s.has(1):
                        b = s.buf(1)
                        for t in range(QT):
                            last = nc.vector.bn_aggr(mean_var[b][:, t, :], stats[b][:, t, :])
                        last.then_inc(mean_set, 1)
                    if s.has(0):
                        b = s.buf(0)
                        dve.wait_ge(hi_split, s.row(1))
                        nc.vector.scalar_tensor_tensor(out=k_lo[b][:], in0=bank_qk[:, T:2 * T], scalar=qkv_bias[:, 1:2],
                                                       in1=k_hi[b][:].bitcast(F32), op0=ALU.add, op1=ALU.subtract)
                        for h in range(H):
                            rows = slice(HD * h, HD * (h + 1))
                            last = nc.vector.scalar_tensor_tensor(out=q_lo[b][rows, h, :], in0=bank_qk[rows, 0:T], scalar=qkv_bias[rows, 0:1],
                                                                  in1=q_hi[b][rows, h, :].bitcast(F32), op0=ALU.add, op1=ALU.subtract)
                        last.then_inc(lo_split, 1)
                    for h in range(H):
                        if s.has(0):
                            b = s.buf(0)
                            dve.wait_ge(s_done, s.row(0) * H + (h + 1))
                            nc.vector.tensor_reduce(row_max[b][:, :, h], bank_s[:].rearrange("p (t k) -> p t k", t=QT),
                                                    AX_X, ALU.max).then_inc(row_max_set, 1)
                        if s.has(1) and h == 1:
                            b = s.buf(1)
                            dve.wait_ge(rstd_set, s.row(2))
                            wait(dve, zT_done, s.row(0))
                            for t in range(QT):
                                last = nc.vector.tensor_scalar(xn[b][:, t, :], x_in[b][:, t, :], mean_var[b][:, t, 0:1], rstd[b][:, t:t + 1],
                                                               ALU.subtract, ALU.mult)
                            last.then_inc(xn_set, 1)
                    if s.has(0):
                        b = s.buf(0)
                        dve.wait_ge(row_max_set, s.row(1) * H)
                        nc.vector.tensor_copy(max_hl[b][:, :, :, 0], row_max[b][:]).then_inc(max_hi_set, 1)
                        dve.wait_ge(max_hi_set, s.row(1))
                        nc.vector.tensor_tensor(max_hl[b][:, :, :, 1], row_max[b][:], max_hl[b][:, :, :, 0], ALU.subtract).then_inc(max_split, 1)

                all_slots(dve, slot)

            @block.scalar
            def _(act):
                act.wait_ge(folded_b, 1)
                act.wait_ge(consts_set, 1)

                def slot(act, s):
                    def exps(u):
                        pair, t = u // QT, u % QT
                        act.wait_ge(sT_done, s.row(-1) * UNITS + (u + 1))
                        wait(act, pv_done, s.row(-1) * H + (2 * pair - 2))
                        nc.scalar.activation(pT[pair][:, t, :, :].rearrange("p h q -> p (h q)"), bank_sT[t][:], ACT.Exp, scale=SCALE).then_inc(p_set, 1)

                    if s.has(0):
                        act.wait_ge(zT_done, s.row(1))
                        wait(act, v_done, s.row(0))
                        nc.scalar.activation(zT[:], bank_T[:, 0:T], ACT.Identity).then_inc(zT_copied, 1)
                    if s.has(-1):
                        act.wait_ge(maxT_done, s.row(0))
                        wait(act, sT_done, s.row(-1) * UNITS)
                        nc.scalar.activation(neg_max[:], bank_qk[:, 0:T], ACT.Copy, scale=-1.0).then_inc(neg_max_set, 1)
                        exps(0)
                    if s.has(-2):
                        act.wait_ge(attT_done, s.row(-1))
                        wait(act, proj_done, s.row(-2))
                        nc.scalar.activation(attT[:], bank_T[:, 0:T], ACT.Identity).then_inc(attT_copied, 1)
                    if s.has(-1):
                        exps(1)
                    if s.has(0):
                        b = s.buf(0)
                        act.wait_ge(qk_done, s.row(1))
                        wait(act, sT_done, s.row(-1) * UNITS)
                        for h in range(H):
                            rows = slice(HD * h, HD * (h + 1))
                            nc.scalar.activation(q_hi[b][rows, h, :], bank_qk[rows, 0:T], ACT.Identity, bias=qkv_bias[rows, 0:1])
                        nc.scalar.activation(k_hi[b][:], bank_qk[:, T:2 * T], ACT.Identity, bias=qkv_bias[:, 1:2]).then_inc(hi_split, 1)
                    if s.has(-1):
                        exps(2)
                    if s.has(0):
                        act.wait_ge(v_done, s.row(1))
                        wait(act, pv_done, s.row(-1) * H)
                        nc.scalar.activation(v_one[b][:, :, :, 0:HD], bank_v[:, 0:QT * D].rearrange("p (t h d) -> p t h d", t=QT, h=H),
                                             ACT.Identity).then_inc(v_copied, 1)
                    if s.has(-1):
                        exps(3)

                all_slots(act, slot)

            @block.tensor
            def _(pe):
                pe.wait_ge(consts_set, H + 2)
                pe.wait_ge(w_loaded, 8 * 16)
                for i in range(3):
                    last = nc.tensor.matmul(bank_T[:, i:i + 1], w_raw[:, i * D:(i + 1) * D], b_col[:], start=True, stop=True)
                last.then_inc(folded_mm, 1)
                pe.wait_ge(folded_b, 2)
                nc.tensor.matmul(bank_T[:, 0:D], v_bias_wide[:], wp[:], start=True, stop=True).then_inc(folded_mm, 1)
                pe.wait_ge(folded_b, 3)

                def slot(pe, s):
                    b, a = s.buf(0), s.buf(-1)

                    def scoresT(u):
                        pair, t = u // QT, u % QT
                        wait(pe, p_set, s.row(-1) * UNITS + (u - 1))
                        keys, heads = slice(t * P, (t + 1) * P), slice(2 * pair, 2 * pair + 2)
                        qh, ql = (m[a][:, heads, :].rearrange("p h q -> p (h q)") for m in (q_hi, q_lo))
                        nc.tensor.matmul(bank_sT[t][:], k_hi[a][:, keys], qh, start=True, stop=False)
                        nc.tensor.matmul(bank_sT[t][:], k_lo[a][:, keys], qh, start=False, stop=False)
                        pe.wait_ge(neg_max_set, s.row(0))
                        for i in range(2):
                            nc.tensor.matmul(bank_sT[t][:, i * T:(i + 1) * T], head_rows[:, 2 * pair + i, :], neg_max[:], start=False, stop=False)
                        last = nc.tensor.matmul(bank_sT[t][:], k_hi[a][:, keys], ql, start=False, stop=True)
                        last.then_inc(sT_done, 1)

                    def weighted(h):
                        pe.wait_ge(p_set, s.row(-1) * UNITS + (h // 2 + 1) * QT)
                        heads = slice(FIRST_HEAD[h], FIRST_HEAD[h] + WIDE)
                        for q in range(QT):
                            for t in range(QT):
                                last = nc.tensor.matmul(banks_o[:, q, h * O_COLS:(h + 1) * O_COLS], pT[h // 2][:, t, h % 2, q * P:(q + 1) * P],
                                                        v_one[a][:, t, heads, :].rearrange("p h d -> p (h d)"),
                                                        start=(t == 0), stop=(t == QT - 1))
                        last.then_inc(pv_done, 1)

                    def scores(h):
                        wait(pe, row_max_set, s.row(0) * H + h)
                        for t in range(QT):
                            last = nc.tensor.matmul(bank_s[:, t * T:(t + 1) * T], q_hi[b][:, h, t * P:(t + 1) * P], k_hi[b][:], start=True, stop=True)
                        last.then_inc(s_done, 1)

                    if s.has(0):
                        pe.wait_ge(xn_set, s.row(1))
                        wait(pe, attT_copied, s.row(-2))
                        for t in range(QT):
                            last = nc.tensor.transpose(bank_T[:, t * P:(t + 1) * P], xn[b][:, t, :], ident[:])
                        last.then_inc(zT_done, 1)
                    if s.has(-1):
                        pe.wait_ge(max_split, s.row(0))
                        pe.wait_ge(lo_split, s.row(0))
                        for t in range(QT):
                            last = nc.tensor.matmul(bank_qk[:, t * P:(t + 1) * P], max_hl[a][:, t, :, :].rearrange("p h d -> p (h d)"), ident_bf[:], start=True, stop=True)
                        last.then_inc(maxT_done, 1)
                        scoresT(0)
                    if s.has(-2):
                        pe.wait_ge(att_set, s.row(-1))
                        if s.has(0):
                            pe.wait_ge(zT_copied, s.row(1))
                        for t in range(QT):
                            last = nc.tensor.transpose(bank_T[:, t * P:(t + 1) * P], att[:, t, :, :].rearrange("p h d -> p (h d)"), ident[:])
                        last.then_inc(attT_done, 1)
                    if s.has(-1):
                        scoresT(1)
                    if s.has(0):
                        pe.wait_ge(zT_copied, s.row(1))
                        for i in range(2):
                            last = nc.tensor.matmul(bank_qk[:, i * T:(i + 1) * T], w[:, i * D:(i + 1) * D], zT[:], start=True, stop=True)
                        last.then_inc(qk_done, 1)
                    if s.has(-2):
                        pe.wait_ge(attT_copied, s.row(-1))
                        if s.has(-1):
                            pe.wait_ge(v_copied, s.row(0))
                        for t in range(QT):
                            last = nc.tensor.matmul(bank_v[:, t * D:(t + 1) * D], attT[:, t * P:(t + 1) * P], wp[:], start=True, stop=True)
                        last.then_inc(proj_done, 1)
                    if s.has(-1):
                        if not s.has(-2):
                            pe.wait_ge(v_copied, s.row(0))
                        scoresT(2)
                    if s.has(0):
                        wait(pe, y_set, s.row(-1))
                        wait(pe, v_copied, s.row(0))
                        for t in range(QT):
                            last = nc.tensor.matmul(bank_v[:, t * D:(t + 1) * D], zT[:, t * P:(t + 1) * P], w[:, 2 * D:3 * D], start=True, stop=True)
                        last.then_inc(v_done, 1)
                        pe.wait_ge(hi_split, s.row(1))
                        scores(0)
                    if s.has(-1):
                        scoresT(3)
                    for h in range(H):
                        if s.has(-1):
                            weighted(h)
                        if s.has(0) and h < H - 1:
                            scores(h + 1)

                all_slots(pe, slot)


def triangle_projections(nc, outgoing, x, ab, gate, ln_w, ln_b, w_parts, b_parts):
    L, T, D = x.shape
    JT = T // P
    CB = ab.shape[4]
    NCB = ab.shape[2]
    GI = 2
    SI = 16
    G = L // GI
    GS = SI // GI
    TILES = GI * JT
    assert D == P and NCB * CB == 2 * D and TILES * P == 512

    x_v = x.rearrange("(s i) (t p) c -> s p t i c", i=SI, p=P) if outgoing else x.rearrange("(t p) (s i) c -> s p t i c", i=SI, p=P)
    ab_v = ab.rearrange("t p n (s i) c -> s t p n (i c)", i=SI)
    gate_v = gate.rearrange("(t p) (s i) c -> s p t i c", i=SI, p=P)

    with ExitStack() as ctx:
        tag = "po_" if outgoing else "pi_"

        def sb(name, shape, dt=F32):
            return ctx.enter_context(nc.sbuf_tensor(tag + name, shape, dt))

        def bank(name):
            return ctx.enter_context(nc.psum_tensor(tag + name, [P, 512], F32))

        def sem(name):
            return ctx.enter_context(nc.semaphore(tag + name))

        NW = 5 * D
        ident, one_col = sb("ident", [P, P]), sb("one_col", [P, 1])
        half_neg, eps = sb("half_neg", [P, JT, GI]), sb("eps", [P, JT, GI])
        g_col, b_col, b_wide, minus_mean = sb("g_col", [P, 1]), sb("b_col", [P, 1]), sb("b_wide", [P, P]), sb("minus_mean", [P, P])
        b_mean = sb("b_mean", [P, P])
        w_raw, w_gain, bias, w_part, w = (sb(n, [P, NW]) for n in ("w_raw", "w_gain", "bias", "w_part", "w"))
        x_in = [sb(f"x_in{i}", [P, JT, SI, D]) for i in range(2)]
        ab_out = [sb(f"ab_out{i}", [P, JT, NCB, SI, CB]) for i in range(2)]
        gate_out = [sb(f"gate_out{i}", [P, JT, SI, D]) for i in range(2)]
        stats = [sb(f"stats{i}", [P, JT, GI, 6]) for i in range(2)]
        mean_var = [sb(f"mean_var{i}", [P, JT, GI, 2]) for i in range(2)]
        var_eps = [sb(f"var_eps{i}", [P, JT, GI]) for i in range(2)]
        rstd = [sb(f"rstd{i}", [P, JT, GI]) for i in range(2)]
        xn = [sb(f"xn{i}", [P, JT, GI, D]) for i in range(2)]
        zT = [sb(f"zT{i}", [P, TILES, P]) for i in range(2)]
        sig = [sb(f"sig{i}", [P, 2 * D]) for i in range(2)]
        bank_T = [bank(f"bank_T{i}") for i in range(2)]
        bank_ab = [bank(f"bank_ab{i}") for i in range(4)]
        bank_g = [bank(f"bank_g{i}") for i in range(2)]

        w_loaded, consts_set, w_gained, w_mm, w_set = (sem(n) for n in ("w_loaded", "consts_set", "w_gained", "w_mm", "w_set"))
        x_loaded, ab_stored, gate_stored = ([sem(f"{n}{i}") for i in range(2)] for n in ("x_loaded", "ab_stored", "gate_stored"))
        stats_set, mean_set, eps_set, rstd_set, xn_set, zT_done, zT_copied, ab_done, sig_set, ab_set, g_done, gate_set = (sem(n) for n in (
            "stats_set", "mean_set", "eps_set", "rstd_set", "xn_set", "zT_done", "zT_copied", "ab_done", "sig_set", "ab_set", "g_done", "gate_set"))

        LOADS = L // SI

        class Slot:

            def __init__(self, it, s0):
                self.it, self.s0, self.loop = it, s0, not isinstance(it, int)

            def has(self, k):
                return self.loop or 0 <= self.s0 + k < G

            def group(self, k):
                return self.it * (2 * GS) + (self.s0 + k)

            def turn(self, k):
                return self.it + (self.s0 + k) // (2 * GS)

            def buf(self, k):
                return (self.s0 + k) // GS % 2

            def pos(self, k):
                return (self.s0 + k) % GS

        def all_slots(slot):
            def run(engine):
                for s in range(-2, 0):
                    slot(Slot(0, s))
                with engine.Fori(0, LOADS // 2 - 1) as it:
                    for s in range(2 * GS):
                        slot(Slot(it, s))
                for s in range(G - 2 * GS, G):
                    slot(Slot(0, s))
            return run

        AB_AHEAD, GATE_AHEAD, G_DONE_AHEAD, STORED_AHEAD = TILES, 2, 1, 1

        with nc.Block() as block:

            @block.sync
            def _(sp):
                sp.dma_start(g_col[:], ln_w.rearrange("(c a) -> c a", a=1)).then_inc(w_loaded, 16)
                sp.dma_start(b_col[:], ln_b.rearrange("(c a) -> c a", a=1)).then_inc(w_loaded, 16)
                for i in range(5):
                    sp.dma_start(w_raw[:, i * D:(i + 1) * D], w_parts[i]).then_inc(w_loaded, 16)
                    sp.dma_start(bias[:, i * D:(i + 1) * D], b_parts[i].rearrange("(a c) -> a c", a=1).to_broadcast([P, D])).then_inc(w_loaded, 16)

                def load(n, buf):
                    for t in range(JT):
                        for half in (slice(0, SI // 2), slice(SI // 2, SI)):
                            sp.dma_start(x_in[buf][:, t, half, :], x_v[n, :, t, half]).then_inc(x_loaded[buf], 16)

                def store(n, buf):
                    sp.wait_ge(ab_set, (n + 1) * (GS * TILES) + AB_AHEAD)
                    for t in range(JT):
                        sp.dma_start(ab_v[n, t], ab_out[buf][:, t, :, :, :].rearrange("p n i c -> p n (i c)")).then_inc(ab_stored[buf], 16)
                    sp.wait_ge(gate_set, (n + 1) * GS + GATE_AHEAD)
                    for t in range(JT):
                        sp.dma_start(gate_v[n, :, t], gate_out[buf][:, t, :, :]).then_inc(gate_stored[buf], 16)

                for n in range(2):
                    load(n, n)
                with sp.Fori(0, LOADS // 2 - 1) as it:
                    for buf in range(2):
                        sp.wait_ge(xn_set, (it * 2 + (buf + 1)) * GS)
                        load(it * 2 + (buf + 2), buf)
                        store(it * 2 + buf, buf)
                for buf in range(2):
                    store(LOADS - 2 + buf, buf)
                for buf in range(2):
                    sp.wait_ge(ab_stored[buf], LOADS // 2 * JT * 16 + STORED_AHEAD)
                    sp.wait_ge(gate_stored[buf], LOADS // 2 * JT * 16 + STORED_AHEAD)

            @block.gpsimd
            def _(pool):
                nc.gpsimd.memset(minus_mean[:], -1.0 / D)
                nc.gpsimd.memset(one_col[:], 1.0)
                nc.gpsimd.memset(half_neg[:], -0.5)
                nc.gpsimd.memset(eps[:], EPS)
                nc.gpsimd.memset(ident[:], 0.0).then_inc(consts_set, 1)
                pool.wait_ge(consts_set, 1)
                nc.gpsimd.affine_select(out=ident[:], in_=ident[:], compare_op=ALU.not_equal, fill=1.0, base=0,
                                        pattern=[[-1, P]], channel_multiplier=1).then_inc(consts_set, 1)

                def slot(s):
                    if s.has(2):
                        b = s.pos(2) % 2
                        pool.wait_ge(mean_set, s.group(3))
                        nc.gpsimd.tensor_tensor(var_eps[b][:], mean_var[b][:, :, :, 1], eps[:], ALU.add).then_inc(eps_set, 1)
                        pool.wait_ge(eps_set, s.group(3))
                        nc.gpsimd.tensor_tensor(rstd[b][:], var_eps[b][:], half_neg[:], ALU.pow).then_inc(rstd_set, 1)

                all_slots(slot)(pool)

            @block.vector
            def _(dve):
                dve.sem_inc(ab_set, AB_AHEAD)
                for buf in range(2):
                    dve.sem_inc(ab_stored[buf], STORED_AHEAD)
                dve.wait_ge(w_loaded, 12 * 16)
                nc.vector.tensor_copy(b_wide[:], b_col[:, 0:1].to_broadcast([P, P])).then_inc(w_gained, 1)
                nc.vector.tensor_scalar(w_gain[:], w_raw[:], g_col[:, 0:1], None, ALU.mult).then_inc(w_gained, 1)
                dve.wait_ge(w_gained, 2)
                nc.vector.tensor_scalar(b_mean[:], b_wide[:], 1.0 / D, None, ALU.mult).then_inc(w_gained, 1)
                nc.vector.scalar_tensor_tensor(out=w_part[:], in0=bias[:], scalar=1.0 / D, in1=w_gain[:], op0=ALU.mult, op1=ALU.add).then_inc(w_gained, 1)
                dve.wait_ge(w_gained, 4)
                dve.wait_ge(w_mm, 1)
                nc.vector.tensor_tensor(w[:, 0:4 * D], bank_ab[0][:], w_part[:, 0:4 * D], ALU.add)
                nc.vector.tensor_tensor(w[:, 4 * D:NW], bank_ab[1][:, 0:D], w_part[:, 4 * D:NW], ALU.add).then_inc(w_set, 1)

                def slot(s):
                    def gated(tile):
                        dve.wait_ge(sig_set, s.group(0) * TILES + (tile + 1))
                        t, i = tile // GI, tile % GI
                        nc.vector.tensor_tensor(ab_out[s.buf(0)][:, t, :, s.pos(0) * GI + i, :],
                                                bank_ab[tile][:, 2 * D:4 * D].rearrange("p (n c) -> p n c", c=CB),
                                                sig[tile % 2][:].rearrange("p (n c) -> p n c", c=CB), ALU.mult).then_inc(ab_set, 1)

                    if s.has(2):
                        b = s.pos(2) % 2
                        if s.pos(2) == 0:
                            dve.wait_ge(x_loaded[s.buf(2)], (s.turn(2) + 1) * (2 * 16 * JT))
                        for t in range(JT):
                            for i in range(GI):
                                last = nc.vector.bn_stats(stats[b][:, t, i, :], x_in[s.buf(2)][:, t, s.pos(2) * GI + i, :])
                        last.then_inc(stats_set, 1)
                        dve.wait_ge(stats_set, s.group(3))
                    if s.has(0):
                        if s.pos(0) == 0:
                            dve.wait_ge(ab_stored[s.buf(0)], s.turn(0) * (16 * JT) + STORED_AHEAD)
                        gated(0)
                    if s.has(2):
                        for t in range(JT):
                            for i in range(GI):
                                last = nc.vector.bn_aggr(mean_var[b][:, t, i, :], stats[b][:, t, i, :])
                        last.then_inc(mean_set, 1)
                    if s.has(0):
                        for tile in range(1, TILES):
                            gated(tile)
                    if s.has(2):
                        dve.wait_ge(rstd_set, s.group(3))
                        if s.has(0):
                            dve.wait_ge(zT_done, s.group(1))
                        for t in range(JT):
                            for i in range(GI):
                                last = nc.vector.tensor_scalar(xn[b][:, t, i, :], x_in[s.buf(2)][:, t, s.pos(2) * GI + i, :],
                                                               mean_var[b][:, t, i, 0:1], rstd[b][:, t, i:i + 1], ALU.subtract, ALU.mult)
                        last.then_inc(xn_set, 1)

                all_slots(slot)(dve)

            @block.scalar
            def _(act):
                act.sem_inc(gate_set, GATE_AHEAD)
                for buf in range(2):
                    act.sem_inc(gate_stored[buf], STORED_AHEAD)
                act.wait_ge(consts_set, 1)

                def slot(s):
                    if s.has(1):
                        b = s.pos(1) % 2
                        act.wait_ge(zT_done, s.group(2))
                        if s.has(0):
                            act.wait_ge(g_done, s.group(0) + G_DONE_AHEAD)
                        nc.scalar.activation(zT[b][:].rearrange("p a b -> p (a b)"), bank_T[b][:], ACT.Identity, bias=one_col[:, 0:1]).then_inc(zT_copied, 1)
                    if s.has(0):
                        for tile in range(TILES):
                            act.wait_ge(ab_done, s.group(0) * TILES + (tile + 1))
                            act.wait_ge(ab_set, s.group(0) * TILES + (tile - 1 + AB_AHEAD))
                            nc.scalar.activation(sig[tile % 2][:], bank_ab[tile][:, 0:2 * D], ACT.Sigmoid).then_inc(sig_set, 1)
                        act.wait_ge(g_done, s.group(1) + G_DONE_AHEAD)
                        if s.pos(0) == 0:
                            act.wait_ge(gate_stored[s.buf(0)], s.turn(0) * (16 * JT) + STORED_AHEAD)
                        nc.scalar.activation(gate_out[s.buf(0)][:, :, s.pos(0) * GI:(s.pos(0) + 1) * GI, :],
                                             bank_g[s.pos(0) % 2][:].rearrange("p (t i c) -> p t i c", t=JT, i=GI), ACT.Sigmoid).then_inc(gate_set, 1)

                all_slots(slot)(act)

            @block.tensor
            def _(pe):
                pe.sem_inc(g_done, G_DONE_AHEAD)
                pe.wait_ge(consts_set, 2)
                pe.wait_ge(w_gained, 4)
                for bank_w, cols in ((bank_ab[0], slice(0, 4 * D)), (bank_ab[1], slice(4 * D, NW))):
                    out = bank_w[:, 0:cols.stop - cols.start]
                    nc.tensor.matmul(out, minus_mean[:], w_gain[:, cols], start=True, stop=False)
                    last = nc.tensor.matmul(out, b_mean[:], w_raw[:, cols], start=False, stop=True)
                last.then_inc(w_mm, 1)
                pe.wait_ge(w_set, 1)

                def slot(s):
                    if s.has(0):
                        pe.wait_ge(zT_copied, s.group(1))
                    if s.has(1):
                        b = s.pos(1) % 2
                        pe.wait_ge(xn_set, s.group(2))
                        for t in range(JT):
                            for i in range(GI):
                                last = nc.tensor.transpose(bank_T[b][:, (t * GI + i) * P:(t * GI + i + 1) * P], xn[b][:, t, i, :], ident[:])
                        last.then_inc(zT_done, 1)
                    if s.has(0):
                        b = s.pos(0) % 2
                        for tile in range(TILES):
                            pe.wait_ge(ab_set, s.group(0) * TILES + (tile + 1 - TILES + AB_AHEAD))
                            nc.tensor.matmul(bank_ab[tile][:], zT[b][:, tile, :], w[:, 0:4 * D], start=True, stop=True).then_inc(ab_done, 1)
                        pe.wait_ge(gate_set, s.group(0) + (GATE_AHEAD - 1))
                        for tile in range(TILES):
                            last = nc.tensor.matmul(bank_g[b][:, tile * D:(tile + 1) * D], zT[b][:, tile, :], w[:, 4 * D:NW], start=True, stop=True)
                        last.then_inc(g_done, 1)

                all_slots(slot)(pe)


def triangle_product(nc, outgoing, x, x_out, ab, gate, ln_w, ln_b, w_z, b_z):
    L, T, D = x.shape
    JT, _, NCB, _, CB = ab.shape
    NB = NCB // 2
    HALVES = L // P
    QUARTERS = HALVES * HALVES
    GK = 4
    EG = P // GK
    SLOTS = EG // NB * 2
    ITS = NB // 2
    PAIRS = SLOTS // 2
    BH = CB // 4
    assert SLOTS == 4 and BH == 2 and GK * P == 512

    ab_v = ab.rearrange("t p n i c -> n p t (i c)")
    x_v = x.rearrange("(h p) (f k) c -> h f p k c", p=P, k=2 * GK)
    out_v = x_out.rearrange("(h p) (f k) c -> h f p k c", p=P, k=2 * GK)
    gate_v = gate.rearrange("(f k) (h p) c -> h f p k c", p=P, k=2 * GK) if outgoing else gate.rearrange("(h p) (f k) c -> h f p k c", p=P, k=2 * GK)

    with ExitStack() as ctx:
        tag = "to_" if outgoing else "ti_"

        def sb(name, shape, dt=F32):
            return ctx.enter_context(nc.sbuf_tensor(tag + name, shape, dt))

        def bank(name):
            return ctx.enter_context(nc.psum_tensor(tag + name, [P, 512], F32))

        def sem(name):
            return ctx.enter_context(nc.semaphore(tag + name))

        ident, one_col = sb("ident", [P, P]), sb("one_col", [P, 1])
        half_neg, eps = sb("half_neg", [P, GK]), sb("eps", [P, GK])
        g_col, b_col = sb("g_col", [P, 1]), sb("b_col", [P, 1])
        w = sb("w", [P, D])
        a_in = [sb(f"a_in{i}", [P, JT, P, CB]) for i in range(2)]
        b_in = [sb(f"b_in{i}", [P, JT, P, CB]) for i in range(2)]
        p_acc = [sb(f"p_acc{i}", [P, P, D]) for i in range(2)]
        stats = [sb(f"stats{i}", [P, GK, 6]) for i in range(2)]
        mean_var = [sb(f"mean_var{i}", [P, GK, 2]) for i in range(2)]
        var_eps = [sb(f"var_eps{i}", [P, GK]) for i in range(2)]
        rstd = [sb(f"rstd{i}", [P, GK]) for i in range(2)]
        pn = [sb(f"pn{i}", [P, GK, D]) for i in range(2)]
        pT = [sb(f"pT{i}", [P, GK, P]) for i in range(2)]
        gated = [sb(f"gated{i}", [P, GK, D]) for i in range(2)]
        x_res = [sb(f"x_res{i}", [P, 2 * GK, D]) for i in range(2)]
        g_in = [sb(f"g_in{i}", [P, 2 * GK, D]) for i in range(2)]
        y = [sb(f"y{i}", [P, 2 * GK, D]) for i in range(2)]
        w_raw, w_gain, bias, w_part = (y[0][:, i, :] for i in range(4))
        b_wide, b_mean, minus_mean = (y[0][:, 4 + i, :] for i in range(3))
        bank_p = [bank(f"bank_p{i}") for i in range(2 * BH)]
        bank_T = [bank(f"bank_T{i}") for i in range(2)]
        bank_z = [bank(f"bank_z{i}") for i in range(2)]

        w_loaded, consts_set, w_gained, w_mm, w_set = (sem(n) for n in ("w_loaded", "consts_set", "w_gained", "w_mm", "w_set"))
        ab_loaded, xg_loaded, y_stored = ([sem(f"{n}{i}") for i in range(2)] for n in ("ab_loaded", "xg_loaded", "y_stored"))
        p_done, p_copied, stats_set, mean_set, eps_set, rstd_set, pn_set, pT_done, pT_copied, z_done, gated_set, y_set = (sem(n) for n in (
            "p_done", "p_copied", "stats_set", "mean_set", "eps_set", "rstd_set", "pn_set", "pT_done", "pT_copied", "z_done", "gated_set", "y_set"))

        P_AHEAD, GATED_AHEAD, Z_AHEAD, Y_AHEAD, STORED_AHEAD = 2 * BH, 2, 1, 2, 1

        class Slot:

            def __init__(self, quarter, it, j):
                self.quarter, self.it, self.j = quarter, it, j
                self.last = isinstance(it, int) and it == ITS - 1

            def group(self, k):
                return self.it * SLOTS + ((self.quarter - 1) * EG + self.j + k)

            def has(self, k):
                return not (self.quarter == QUARTERS and self.last and self.j + k >= SLOTS)

            def place(self, k):
                if self.last and self.j + k >= SLOTS:
                    return self.quarter % 2, (self.j + k - SLOTS) * GK
                return (self.quarter - 1) % 2, self.it * (SLOTS * GK) + (self.j + k) * GK

        def banks_of(it, j):
            if isinstance(it, int):
                return range(2 * j, 2 * j + 2) if j < SLOTS // 2 else ()
            return (j,)

        def steps(engine, slot, first):
            for quarter in range(first, QUARTERS + 1):
                with engine.Fori(0, ITS - 1) as it:
                    for j in range(SLOTS):
                        slot(quarter, it, j)
                for j in range(SLOTS):
                    slot(quarter, ITS - 1, j)
                yield quarter

        with nc.Block() as block:

            @block.sync
            def _(sp):
                sp.dma_start(g_col[:], ln_w.rearrange("(c a) -> c a", a=1)).then_inc(w_loaded, 16)
                sp.dma_start(b_col[:], ln_b.rearrange("(c a) -> c a", a=1)).then_inc(w_loaded, 16)
                sp.dma_start(w_raw, w_z).then_inc(w_loaded, 16)
                sp.dma_start(bias, b_z.rearrange("(a c) -> a c", a=1).to_broadcast([P, D])).then_inc(w_loaded, 16)

                def load_ab(quarter, block_at, buf):
                    ih, kh = quarter // HALVES, quarter % HALVES
                    n = P * CB
                    sp.dma_start(a_in[buf][:].rearrange("p t i c -> p t (i c)"), ab_v[block_at, :, :, ih * n:(ih + 1) * n]).then_inc(ab_loaded[buf], 16)
                    sp.dma_start(b_in[buf][:].rearrange("p t i c -> p t (i c)"), ab_v[block_at + NB, :, :, kh * n:(kh + 1) * n]).then_inc(ab_loaded[buf], 16)

                def load_xg(quarter, pair, buf):
                    ih, kh = quarter // HALVES, quarter % HALVES
                    sp.dma_start(x_res[buf][:], x_v[ih, pair + kh * (EG // 2)]).then_inc(xg_loaded[buf], 16)
                    sp.dma_start(g_in[buf][:], gate_v[ih, pair + kh * (EG // 2)]).then_inc(xg_loaded[buf], 16)

                for buf in range(2):
                    load_ab(0, buf, buf)
                    load_xg(0, buf, buf)

                def slot(quarter, it, j):
                    if j % 2:
                        return
                    buf = j // 2
                    last = isinstance(it, int) and it == ITS - 1
                    if quarter < QUARTERS and not (last and quarter == QUARTERS - 1):
                        sp.wait_ge(p_done, it * (2 * BH) + (quarter * NB + buf + 1) * BH)
                        if last:
                            load_ab(quarter + 1, buf, buf)
                        else:
                            load_ab(quarter, it * 2 + (buf + 2), buf)
                    if quarter > 0:
                        sp.wait_ge(y_set, it * SLOTS + ((quarter - 1) * EG + j + 2 + Y_AHEAD))
                        ih, kh = (quarter - 1) // HALVES, (quarter - 1) % HALVES
                        sp.dma_start(out_v[ih, it * PAIRS + (kh * (EG // 2) + buf)], y[buf][:]).then_inc(y_stored[buf], 16)
                        if not last:
                            load_xg(quarter - 1, it * PAIRS + (buf + 2), buf)
                        elif quarter < QUARTERS:
                            load_xg(quarter, buf, buf)

                for _ in steps(sp, slot, 0):
                    pass
                for buf in range(2):
                    sp.wait_ge(y_stored[buf], QUARTERS * ITS * 16 + STORED_AHEAD)

            @block.gpsimd
            def _(pool):
                pool.sem_inc(y_set, Y_AHEAD)
                for buf in range(2):
                    pool.sem_inc(y_stored[buf], STORED_AHEAD)
                nc.gpsimd.memset(minus_mean, -1.0 / D)
                nc.gpsimd.memset(one_col[:], 1.0)
                nc.gpsimd.memset(half_neg[:], -0.5)
                nc.gpsimd.memset(eps[:], EPS)
                nc.gpsimd.memset(ident[:], 0.0).then_inc(consts_set, 1)
                pool.wait_ge(consts_set, 1)
                nc.gpsimd.affine_select(out=ident[:], in_=ident[:], compare_op=ALU.not_equal, fill=1.0, base=0,
                                        pattern=[[-1, P]], channel_multiplier=1).then_inc(consts_set, 1)

                def power(b, count):
                    pool.wait_ge(mean_set, count)
                    nc.gpsimd.tensor_tensor(var_eps[b][:], mean_var[b][:, :, 1], eps[:], ALU.add).then_inc(eps_set, 1)
                    pool.wait_ge(eps_set, count)
                    nc.gpsimd.tensor_tensor(rstd[b][:], var_eps[b][:], half_neg[:], ALU.pow).then_inc(rstd_set, 1)

                for e in range(2):
                    power(e, e + 1)
                pool.wait_ge(w_set, 1)

                def slot(quarter, it, j):
                    s = Slot(quarter, it, j)
                    if s.has(2):
                        power(j % 2, s.group(3))
                    buf = j // 2
                    if j % 2 == 0:
                        turn = it + (quarter - 1) * ITS
                        pool.wait_ge(y_stored[buf], turn * 16 + STORED_AHEAD)
                        pool.wait_ge(xg_loaded[buf], (turn + 1) * 32)
                    pool.wait_ge(gated_set, s.group(1) + GATED_AHEAD)
                    cols = slice((j % 2) * GK, (j % 2 + 1) * GK)
                    nc.gpsimd.tensor_tensor(y[buf][:, cols, :], gated[j % 2][:], x_res[buf][:, cols, :], ALU.add).then_inc(y_set, 1)

                for _ in steps(pool, slot, 1):
                    pass

            @block.vector
            def _(dve):
                dve.sem_inc(gated_set, GATED_AHEAD)
                dve.wait_ge(w_loaded, 4 * 16)
                nc.vector.tensor_copy(b_wide, b_col[:, 0:1].to_broadcast([P, P])).then_inc(w_gained, 1)
                nc.vector.tensor_scalar(w_gain, w_raw, g_col[:, 0:1], None, ALU.mult).then_inc(w_gained, 1)
                dve.wait_ge(w_gained, 2)
                nc.vector.tensor_scalar(b_mean, b_wide, 1.0 / D, None, ALU.mult).then_inc(w_gained, 1)
                nc.vector.scalar_tensor_tensor(out=w_part, in0=bias, scalar=1.0 / D, in1=w_gain, op0=ALU.mult, op1=ALU.add).then_inc(w_gained, 1)
                dve.wait_ge(w_gained, 4)
                dve.wait_ge(w_mm, 1)
                nc.vector.tensor_tensor(w[:], bank_z[0][:, 0:D], w_part, ALU.add).then_inc(w_set, 1)

                def column(buf, k0, k):
                    at = k0 + k
                    return p_acc[buf][:, at, :] if isinstance(at, int) else p_acc[buf][:, bass.ds(at, 1), :].rearrange("p a c -> p (a c)")

                def statistics(b, place, count):
                    for k in range(GK):
                        last = nc.vector.bn_stats(stats[b][:, k, :], column(*place, k))
                    last.then_inc(stats_set, 1)
                    dve.wait_ge(stats_set, count)

                def aggregate(b):
                    for k in range(GK):
                        last = nc.vector.bn_aggr(mean_var[b][:, k, :], stats[b][:, k, :])
                    last.then_inc(mean_set, 1)

                def normalise(b, place, count):
                    dve.wait_ge(rstd_set, count)
                    for k in range(GK):
                        last = nc.vector.tensor_scalar(pn[b][:, k, :], column(*place, k), mean_var[b][:, k, 0:1], rstd[b][:, k:k + 1],
                                                       ALU.subtract, ALU.mult)
                    last.then_inc(pn_set, 1)

                dve.wait_ge(p_copied, NB * BH + P_AHEAD)
                for e in range(2):
                    statistics(e, (0, e * GK), e + 1)
                    aggregate(e)
                normalise(0, (0, 0), 1)

                def slot(quarter, it, j):
                    s = Slot(quarter, it, j)
                    b = j % 2
                    if s.has(2):
                        if s.last and j + 2 == SLOTS:
                            dve.wait_ge(p_copied, (quarter + 1) * NB * BH + P_AHEAD)
                        statistics(b, s.place(2), s.group(3))
                    dve.wait_ge(z_done, s.group(1) + Z_AHEAD)
                    if j % 2 == 0:
                        dve.wait_ge(xg_loaded[j // 2], (it + ((quarter - 1) * ITS + 1)) * 32)
                    dve.wait_ge(y_set, s.group(-1) + Y_AHEAD)
                    cols = slice((j % 2) * GK, (j % 2 + 1) * GK)
                    nc.vector.tensor_tensor(gated[b][:].rearrange("p k c -> p (k c)"), bank_z[b][:], g_in[j // 2][:, cols, :].rearrange("p k c -> p (k c)"),
                                            ALU.mult).then_inc(gated_set, 1)
                    if s.has(2):
                        aggregate(b)
                    if s.has(1):
                        dve.wait_ge(pT_done, s.group(1))
                        normalise(1 - b, s.place(1), s.group(2))

                for _ in steps(dve, slot, 1):
                    pass

            @block.scalar
            def _(act):
                act.sem_inc(p_copied, P_AHEAD)
                act.wait_ge(consts_set, 1)

                def gather(quarter, it, j):
                    n = it * (2 * BH) + (quarter * NB * BH + j)
                    act.wait_ge(p_done, n + 1)
                    c0 = (j // BH) * CB + (j % BH) * 4 + it * (2 * CB)
                    cols = slice(c0, c0 + 4) if isinstance(c0, int) else bass.ds(c0, 4)
                    nc.scalar.activation(p_acc[quarter % 2][:, :, cols].rearrange("p k c -> p c k"), bank_p[j][:].rearrange("p (c k) -> p c k", c=4),
                                         ACT.Identity).then_inc(p_copied, 1)

                def copy(b, count):
                    act.wait_ge(pT_done, count)
                    nc.scalar.activation(pT[b][:].rearrange("p a b -> p (a b)"), bank_T[b][:], ACT.Identity, bias=one_col[:, 0:1]).then_inc(pT_copied, 1)

                def slot(quarter, it, j):
                    if quarter < QUARTERS:
                        for j_bank in banks_of(it, j):
                            gather(quarter, it, j_bank)
                    if quarter > 0:
                        s = Slot(quarter, it, j)
                        if s.has(1):
                            act.wait_ge(z_done, s.group(0) + Z_AHEAD)
                            copy(1 - j % 2, s.group(2))

                for quarter in steps(act, slot, 0):
                    if quarter == 0:
                        copy(0, 1)

            @block.tensor
            def _(pe):
                pe.sem_inc(z_done, Z_AHEAD)
                pe.wait_ge(consts_set, 2)
                pe.wait_ge(w_gained, 4)
                nc.tensor.matmul(bank_z[0][:, 0:D], minus_mean, w_gain, start=True, stop=False)
                nc.tensor.matmul(bank_z[0][:, 0:D], b_mean, w_raw, start=False, stop=True).then_inc(w_mm, 1)
                pe.wait_ge(w_set, 1)

                def products(quarter, it, j):
                    buf, half = j // BH, j % BH
                    if half == 0:
                        pe.wait_ge(ab_loaded[buf], (it + (quarter * ITS + 1)) * 32)
                    pe.wait_ge(p_copied, it * (2 * BH) + (quarter * NB * BH + j + 1 - 2 * BH + P_AHEAD))
                    for c in range(4):
                        for t in range(JT):
                            last = nc.tensor.matmul(bank_p[j][:, c * P:(c + 1) * P], a_in[buf][:, t, :, half * 4 + c], b_in[buf][:, t, :, half * 4 + c],
                                                    start=(t == 0), stop=(t == JT - 1))
                    last.then_inc(p_done, 1)

                def turn(b, count):
                    pe.wait_ge(pn_set, count)
                    for k in range(GK):
                        last = nc.tensor.transpose(bank_T[b][:, k * P:(k + 1) * P], pn[b][:, k, :], ident[:])
                    last.then_inc(pT_done, 1)

                def slot(quarter, it, j):
                    if quarter < QUARTERS:
                        for j_bank in banks_of(it, j):
                            products(quarter, it, j_bank)
                    if quarter > 0:
                        s = Slot(quarter, it, j)
                        b = j % 2
                        pe.wait_ge(pT_copied, s.group(1))
                        pe.wait_ge(gated_set, s.group(-1) + GATED_AHEAD)
                        for k in range(GK):
                            last = nc.tensor.matmul(bank_z[b][:, k * D:(k + 1) * D], pT[b][:, k, :], w[:], start=True, stop=True)
                        last.then_inc(z_done, 1)
                        if s.has(1):
                            turn(1 - b, s.group(2))

                for quarter in steps(pe, slot, 0):
                    if quarter == 0:
                        turn(0, 1)


def pair_stack(nc, out, x, at_ln_g, at_ln_b, w_qkv, b_qkv, w_proj, b_proj, ln_in_w, ln_in_b, w_ag, b_ag, w_ap, b_ap,
               w_bg, b_bg, w_bp, b_bp, ln_out_w, ln_out_b, w_z, b_z, w_g, b_g):
    x, out = x[0], out[0]
    L, _, D = x.shape
    CB = 8
    x_at = nc.dram_tensor("x_at", (L, L, D), F32, kind="Internal").ap()
    x_mid = nc.dram_tensor("x_mid", (L, L, D), F32, kind="Internal").ap()
    ab = nc.dram_tensor("ab", (L // P, P, 2 * D // CB, L, CB), F32, kind="Internal").ap()
    gate = nc.dram_tensor("gate", (L, L, D), F32, kind="Internal").ap()

    attention_layer(nc, x, x_at, at_ln_g, at_ln_b, w_qkv, b_qkv, w_proj, b_proj)
    for idx, (outgoing, src, dst) in enumerate(((True, x_at, x_mid), (False, x_mid, out))):
        nc.all_engine_barrier()
        triangle_projections(nc, outgoing, src, ab, gate, ln_in_w[idx], ln_in_b[idx],
                             [m[idx] for m in (w_ag, w_bg, w_ap, w_bp, w_g)], [m[idx] for m in (b_ag, b_bg, b_ap, b_bp, b_g)])
        nc.all_engine_barrier()
        triangle_product(nc, outgoing, src, dst, ab, gate, ln_out_w[idx], ln_out_b[idx], w_z[idx], b_z[idx])


_INS = ["x", "L0_conv_ln_g", "L0_conv_ln_b", "L0_conv_w_qkv", "L0_conv_b_qkv", "L0_conv_w_proj", "L0_conv_b_proj",
        "L1_conv_ln_in_w", "L1_conv_ln_in_b", "L1_conv_w_ag", "L1_conv_b_ag", "L1_conv_w_ap", "L1_conv_b_ap",
        "L1_conv_w_bg", "L1_conv_b_bg", "L1_conv_w_bp", "L1_conv_b_bp", "L1_conv_ln_out_w", "L1_conv_ln_out_b",
        "L1_conv_w_z", "L1_conv_b_z", "L1_conv_w_g", "L1_conv_b_g"]


def kernel(**inputs):
    import numpy as np
    import concourse.bacc as bacc
    from concourse.bass_utils import run_bass_kernel_spmd

    nc = bacc.Bacc("TRN2", target_bir_lowering=False, num_devices=1)
    arrays = {f"in_{name}": np.ascontiguousarray(inputs[name]) for name in _INS}
    ins = [nc.dram_tensor(name, a.shape, mybir.dt.from_np(a.dtype), kind="ExternalInput").ap() for name, a in arrays.items()]
    out = nc.dram_tensor("out", arrays["in_x"].shape, F32, kind="ExternalOutput").ap()
    pair_stack(nc, out, *ins)
    return run_bass_kernel_spmd(nc, [arrays], core_ids=[0]).results[0]["out"]
```

```python
import math
from contextlib import ExitStack

import concourse.bass as bass
from concourse import mybir

P = 128
EPS = 1e-5

ALU = mybir.AluOpType
ACT = mybir.ActivationFunctionType
F32 = mybir.dt.float32
F32R = mybir.dt.float32r
BF16 = mybir.dt.bfloat16
AX_X = mybir.AxisListType.X




def attention_layer(nc, x, x_out, ln_g, ln_b, w_qkv, b_qkv, w_proj, b_proj):
    L, T, D = x.shape
    H, HD = 4, D // 4
    QT = T // P
    UNITS = QT * H // 2
    SCALE = 1.0 / math.sqrt(HD)
    assert D == P and QT == 2 and L % 2 == 0

    x_v = x.rearrange("r (p t) c -> r p t c", t=QT)
    out_v = x_out.rearrange("r (p t) c -> r p t c", t=QT)

    with ExitStack() as ctx:
        def sb(name, shape, dt=F32):
            return ctx.enter_context(nc.sbuf_tensor("at_" + name, shape, dt))

        def bank(name):
            return ctx.enter_context(nc.psum_tensor("at_" + name, [P, 512], F32))

        def sem(name):
            return ctx.enter_context(nc.semaphore("at_" + name))

        ident, one_col = sb("ident", [P, P]), sb("one_col", [P, 1])
        ident_bf = sb("ident_bf", [P, P], BF16)
        half_neg, eps = sb("half_neg", [P, QT]), sb("eps", [P, QT])
        g_col, b_col, b_wide = sb("g_col", [P, 1]), sb("b_col", [P, 1]), sb("b_wide", [P, P])
        minus_mean, b_mean = sb("minus_mean", [P, P]), sb("b_mean", [P, P])
        w_raw, w_gain, bias, w_part, w = (sb(n, [P, 3 * D]) for n in ("w_raw", "w_gain", "bias", "w_part", "w"))
        wp, proj_bias = sb("wp", [P, D]), sb("proj_bias", [P, D])
        x_in = [sb(f"x_in{i}", [P, QT, D]) for i in range(2)]
        stats = [sb(f"stats{i}", [P, QT, 6]) for i in range(2)]
        mean_var = [sb(f"mean_var{i}", [P, QT, 2]) for i in range(2)]
        var_eps = [sb(f"var_eps{i}", [P, QT]) for i in range(2)]
        rstd = [sb(f"rstd{i}", [P, QT]) for i in range(2)]
        xn = [sb(f"xn{i}", [P, QT, D]) for i in range(2)]
        zT = [sb(f"zT{i}", [P, T]) for i in range(2)]
        K_LO, K_HI, Q_HI, Q_LO = range(4)
        parts = [sb(f"parts{i}", [P, 4, T], F32R) for i in range(2)]
        KEYS, QUERIES = range(2)
        PARTS, MAX_ROWS = 3 * HD, slice(3 * HD, 4 * HD)
        packed = [sb(f"packed{i}", [P, H, 2, T], F32R) for i in range(4)]
        PACK_DMAS = 2 * H
        v_one = [sb(f"v_one{i}", [P, QT, H, HD + 1]) for i in range(4)]
        row_max = [sb(f"row_max{i}", [P, QT, H]) for i in range(2)]
        max_hl = [sb(f"max_hl{i}", [P, QT, H, HD], BF16) for i in range(2)]
        x_res = [sb(f"x_res{i}", [P, QT, D]) for i in range(2)]
        x_bias = [sb(f"x_bias{i}", [P, QT, D]) for i in range(2)]
        y = [sb(f"y{i}", [P, QT, D]) for i in range(2)]
        pT = [[sb(f"pT{i}{pair}", [P, QT, 2, T]) for pair in range(H // 2)] for i in range(2)]
        recip = sb("recip", [P, QT, H])
        att = sb("att", [P, QT, H, HD])
        attT = sb("attT", [P, T])

        bank_T, bank_kq, bank_v, bank_s = bank("bank_T"), bank("bank_kq"), bank("bank_v"), bank("bank_s")
        bank_sT = [bank(f"bank_sT{i}") for i in range(2)]
        banks_o = ctx.enter_context(nc.psum_tensor("at_banks_o", [P, QT, 512], F32))
        WIDE = H - 1
        FIRST_HEAD = [h // 2 for h in range(H)]
        O_COLS = WIDE * (HD + 1)
        O_OWN = [h * O_COLS + (h - FIRST_HEAD[h]) * (HD + 1) for h in range(H)]

        def own_sums(pair):
            step = O_OWN[2 * pair + 1] - O_OWN[2 * pair]
            return banks_o[:, :, O_OWN[2 * pair]:O_OWN[2 * pair] + 2 * step].rearrange("p t (h d) -> p t h d", h=2)

        w_loaded, consts_set, w_gained, w_mm, w_set = (sem(n) for n in ("w_loaded", "consts_set", "w_gained", "w_mm", "w_set"))
        x_loaded, res_loaded, y_stored = ([sem(f"{n}{i}") for i in range(2)] for n in ("x_loaded", "res_loaded", "y_stored"))
        packed_moved = [sem(f"packed_moved{i}") for i in range(4)]
        (stats_set, mean_set, eps_set, rstd_set, xn_set, zT_done, zT_copied, kq_done, hi_split, lo_split, hi_packed, v_done, v_copied,
         s_done, row_max_set, max_hi_set, max_split, maxT_done, neg_max_set, sT_done, p_set, pv_done, recip_set,
         att_set, attT_done, attT_copied, proj_done, x_bias_set, y_set) = (sem(n) for n in (
            "stats_set", "mean_set", "eps_set", "rstd_set", "xn_set", "zT_done", "zT_copied", "kq_done", "hi_split", "lo_split", "hi_packed",
            "v_done", "v_copied", "s_done", "row_max_set", "max_hi_set", "max_split", "maxT_done", "neg_max_set", "sT_done", "p_set", "pv_done",
            "recip_set", "att_set", "attT_done", "attT_copied", "proj_done", "x_bias_set", "y_set"))

        class Slot:

            def __init__(self, it, s0):
                self.it, self.s0, self.loop = it, s0, not isinstance(it, int)

            def has(self, k):
                return self.loop or 0 <= self.s0 + k < L

            def row(self, k):
                return self.it * 4 + (self.s0 + k)

            def turn(self, k, ring=2):
                return self.it * (4 // ring) + (self.s0 + k) // ring

            def buf(self, k, ring=2):
                return (self.s0 + k) % ring

        AHEAD, BEHIND, LOOP_FROM = 5, 4, 8

        def all_slots(engine, slot):
            for s in range(-AHEAD, LOOP_FROM):
                slot(engine, Slot(0, s))
            n = (L - AHEAD - LOOP_FROM) // 4
            with engine.Fori(0, n) as it:
                for j in range(4):
                    slot(engine, Slot(it, LOOP_FROM + j))
            for s in range(LOOP_FROM + 4 * n, L + BEHIND):
                slot(engine, Slot(0, s))

        def wait(engine, s, value):
            if not isinstance(value, int) or value > 0:
                engine.wait_ge(s, value)

        with nc.Block() as block:

            @block.sync
            def _(sp):
                sp.dma_start(g_col[:], ln_g.rearrange("(c a) -> c a", a=1)).then_inc(w_loaded, 16)
                sp.dma_start(b_col[:], ln_b.rearrange("(c a) -> c a", a=1)).then_inc(w_loaded, 16)
                sp.dma_start(w_raw[:], w_qkv).then_inc(w_loaded, 16)
                sp.dma_start(wp[:], w_proj).then_inc(w_loaded, 16)
                sp.dma_start(bias[:], b_qkv.rearrange("(a c) -> a c", a=1).to_broadcast([P, 3 * D])).then_inc(w_loaded, 16)
                sp.dma_start(proj_bias[:], b_proj.rearrange("(a c) -> a c", a=1).to_broadcast([P, D])).then_inc(w_loaded, 16)

                def slot(sp, s):
                    if s.has(-4):
                        sp.wait_ge(y_set, s.row(-3))
                        sp.dma_start(out_v[s.row(-4)], y[s.buf(-4)][:]).then_inc(y_stored[s.buf(-4)], 16)
                    if s.has(2):
                        b, to = s.buf(2), s.buf(2, 4)
                        sp.wait_ge(lo_split, s.row(3))
                        wait(sp, sT_done, s.row(-1) * UNITS)
                        for h in range(H):
                            for block, first in ((1, K_LO), (2, K_HI)):
                                sp.dma_start(packed[to][HD * block:HD * (block + 1), h, :, :].bitcast(F32),
                                             parts[b][HD * h:HD * (h + 1), first:first + 3:2, :].bitcast(F32)).then_inc(packed_moved[to], 16)
                    if s.has(5):
                        wait(sp, xn_set, s.row(4))
                        sp.dma_start(x_in[s.buf(5)][:], x_v[s.row(5)]).then_inc(x_loaded[s.buf(5)], 16)
                    if s.has(-2):
                        wait(sp, x_bias_set, s.row(-3))
                        sp.dma_start(x_res[s.buf(-2)][:], x_v[s.row(-2)]).then_inc(res_loaded[s.buf(-2)], 16)

                all_slots(sp, slot)
                for i in range(2):
                    sp.wait_ge(y_stored[i], 16 * (L // 2))

            @block.gpsimd
            def _(pool):
                nc.gpsimd.memset(minus_mean[:], -1.0 / D)
                nc.gpsimd.memset(one_col[:], 1.0)
                nc.gpsimd.memset(ident[:], 0.0)
                nc.gpsimd.memset(half_neg[:], -0.5)
                nc.gpsimd.memset(eps[:], EPS)
                for i in range(4):
                    nc.gpsimd.memset(v_one[i][:], 1.0)
                for i in range(2):
                    nc.gpsimd.memset(max_hl[i][:], 0.0)
                nc.gpsimd.memset(ident_bf[:], 0.0).then_inc(consts_set, 1)
                pool.wait_ge(consts_set, 1)
                for i in range(4):
                    last = nc.gpsimd.memset(packed[i][MAX_ROWS].bitcast(F32), 0.0)
                last.then_inc(consts_set, 1)
                pool.wait_ge(consts_set, 2)
                for i in range(4):
                    last = nc.gpsimd.memset(packed[i][PARTS:PARTS + 2, :, KEYS, :].bitcast(F32), 1.0)
                last.then_inc(consts_set, 1)
                pool.wait_ge(consts_set, 3)
                nc.gpsimd.affine_select(out=ident[:], in_=ident[:], compare_op=ALU.not_equal, fill=1.0, base=0,
                                        pattern=[[-1, P]], channel_multiplier=1)
                nc.gpsimd.affine_select(out=ident_bf[:], in_=ident_bf[:], compare_op=ALU.not_equal, fill=1.0, base=0,
                                        pattern=[[-1, P]], channel_multiplier=1).then_inc(consts_set, 1)

                def slot(pool, s):
                    if s.has(-3):
                        b = s.buf(-3)
                        pool.wait_ge(res_loaded[b], (s.turn(-3) + 1) * 16)
                        wait(pool, y_set, s.row(-4))
                        nc.gpsimd.tensor_tensor(x_bias[b][:], x_res[b][:], proj_bias[:].rearrange("p (a c) -> p a c", a=1).to_broadcast([P, QT, D]),
                                                ALU.add).then_inc(x_bias_set, 1)
                    if s.has(4):
                        b = s.buf(4)
                        pool.wait_ge(mean_set, s.row(5))
                        nc.gpsimd.tensor_tensor(var_eps[b][:], mean_var[b][:, :, 1], eps[:], ALU.add).then_inc(eps_set, 1)
                        pool.wait_ge(eps_set, s.row(5))
                        nc.gpsimd.tensor_tensor(rstd[b][:], var_eps[b][:], half_neg[:], ALU.pow).then_inc(rstd_set, 1)

                pool.wait_ge(w_loaded, 6 * 16)
                all_slots(pool, slot)

            @block.vector
            def _(dve):
                dve.wait_ge(w_loaded, 6 * 16)
                nc.vector.tensor_copy(b_wide[:], b_col[:, 0:1].to_broadcast([P, P])).then_inc(w_gained, 1)
                nc.vector.tensor_scalar(w_gain[:], w_raw[:], g_col[:, 0:1], None, ALU.mult).then_inc(w_gained, 1)
                dve.wait_ge(w_gained, 2)
                nc.vector.tensor_scalar(b_mean[:], b_wide[:], 1.0 / D, None, ALU.mult).then_inc(w_gained, 1)
                nc.vector.scalar_tensor_tensor(out=w_part[:], in0=bias[:], scalar=1.0 / D, in1=w_gain[:], op0=ALU.mult, op1=ALU.add).then_inc(w_gained, 1)
                dve.wait_ge(w_gained, 4)
                dve.wait_ge(w_mm, 1)
                nc.vector.tensor_tensor(w[:], bank_kq[:, 0:3 * D], w_part[:], ALU.add).then_inc(w_set, 1)
                dve.wait_ge(consts_set, 1)

                def slot(dve, s):
                    def maximum(h):
                        if s.has(0):
                            dve.wait_ge(s_done, s.row(0) * H + (h + 1))
                            nc.vector.tensor_reduce(row_max[s.buf(0)][:, :, h], bank_s[:].rearrange("p (t k) -> p t k", t=QT),
                                                    AX_X, ALU.max).then_inc(row_max_set, 1)

                    if s.has(-3):
                        dve.wait_ge(pv_done, s.row(-2) * H)
                        for pair in range(H // 2):
                            last = nc.vector.reciprocal(recip[:, :, 2 * pair:2 * pair + 2], own_sums(pair)[:, :, :, HD])
                        last.then_inc(recip_set, 1)
                        dve.wait_ge(recip_set, s.row(-2))
                        wait(dve, attT_done, s.row(-3))
                        for pair in range(H // 2):
                            last = nc.vector.tensor_tensor(att[:, :, 2 * pair:2 * pair + 2, :], own_sums(pair)[:, :, :, 0:HD],
                                                           recip[:, :, 2 * pair:2 * pair + 2].rearrange("p t (h d) -> p t h d", d=1).to_broadcast([P, QT, 2, HD]),
                                                           ALU.mult)
                        last.then_inc(att_set, 1)
                    maximum(0)
                    if s.has(-4):
                        b = s.buf(-4)
                        dve.wait_ge(proj_done, s.row(-3))
                        dve.wait_ge(x_bias_set, s.row(-3))
                        wait(dve, y_stored[b], s.turn(-4) * 16)
                        nc.vector.tensor_tensor(y[b][:], bank_v[:, 0:QT * D].rearrange("p (t c) -> p t c", t=QT), x_bias[b][:],
                                                ALU.add).then_inc(y_set, 1)
                    if s.has(3):
                        b = s.buf(3)
                        dve.wait_ge(rstd_set, s.row(4))
                        wait(dve, zT_done, s.row(2))
                        for t in range(QT):
                            last = nc.vector.tensor_scalar(xn[b][:, t, :], x_in[b][:, t, :], mean_var[b][:, t, 0:1], rstd[b][:, t:t + 1],
                                                           ALU.subtract, ALU.mult)
                        last.then_inc(xn_set, 1)
                    maximum(1)
                    maximum(2)
                    if s.has(2):
                        b = s.buf(2)
                        dve.wait_ge(hi_split, s.row(3))
                        if s.has(0):
                            dve.wait_ge(packed_moved[s.buf(0, 4)], (s.turn(0, 4) + 1) * (16 * PACK_DMAS))
                        nc.vector.tensor_tensor(parts[b][:, K_LO:Q_LO + 1:3, :], bank_kq[:].rearrange("p (a t) -> p a t", a=2),
                                                parts[b][:, K_HI:Q_HI + 1, :].bitcast(F32), ALU.subtract).then_inc(lo_split, 1)
                    if s.has(4):
                        b = s.buf(4)
                        dve.wait_ge(x_loaded[b], (s.turn(4) + 1) * 16)
                        for t in range(QT):
                            last = nc.vector.bn_stats(stats[b][:, t, :], x_in[b][:, t, :])
                        last.then_inc(stats_set, 1)
                        dve.wait_ge(stats_set, s.row(5))
                    maximum(3)
                    if s.has(0):
                        b = s.buf(0)
                        dve.wait_ge(row_max_set, s.row(1) * H)
                        nc.vector.tensor_copy(max_hl[b][:, :, :, 0], row_max[b][:]).then_inc(max_hi_set, 1)
                        dve.wait_ge(max_hi_set, s.row(1))
                        nc.vector.tensor_tensor(max_hl[b][:, :, :, 1], row_max[b][:], max_hl[b][:, :, :, 0], ALU.subtract).then_inc(max_split, 1)
                    if s.has(4):
                        b = s.buf(4)
                        for t in range(QT):
                            last = nc.vector.bn_aggr(mean_var[b][:, t, :], stats[b][:, t, :])
                        last.then_inc(mean_set, 1)

                all_slots(dve, slot)

            @block.scalar
            def _(act):
                act.wait_ge(consts_set, 4)

                def slot(act, s):
                    def exps(u):
                        if s.has(-1):
                            pair, t = u // QT, u % QT
                            act.wait_ge(sT_done, s.row(-1) * UNITS + (u + 1))
                            wait(act, pv_done, s.row(-2) * H)
                            nc.scalar.activation(pT[s.buf(-1)][pair][:, t, :, :].rearrange("p h q -> p (h q)"), bank_sT[t][:], ACT.Exp,
                                                 scale=SCALE).then_inc(p_set, 1)

                    if s.has(-1):
                        act.wait_ge(maxT_done, s.row(0))
                        for h in range(H):
                            last = nc.scalar.activation(packed[s.buf(-1, 4)][MAX_ROWS, h, QUERIES, :], bank_kq[HD * h:HD * (h + 1), 0:T], ACT.Copy, scale=-1.0)
                        last.then_inc(neg_max_set, 1)
                    if s.has(1):
                        act.wait_ge(hi_split, s.row(2))
                        wait(act, sT_done, s.row(-2) * UNITS)
                        for h in range(H):
                            last = nc.scalar.activation(packed[s.buf(1, 4)][0:HD, h, :, :].rearrange("p a t -> p (a t)"),
                                                        parts[s.buf(1)][HD * h:HD * (h + 1), K_HI:Q_HI + 1, :].bitcast(F32).rearrange("p a t -> p (a t)"), ACT.Identity)
                        last.then_inc(hi_packed, 1)
                    if s.has(2):
                        act.wait_ge(kq_done, s.row(3))
                        wait(act, hi_packed, s.row(1))
                        if s.has(0):
                            act.wait_ge(packed_moved[s.buf(0, 4)], (s.turn(0, 4) + 1) * (16 * PACK_DMAS))
                        nc.scalar.activation(parts[s.buf(2)][:, K_HI:Q_HI + 1, :].rearrange("p a t -> p (a t)"), bank_kq[:], ACT.Identity).then_inc(hi_split, 1)
                    exps(0)
                    if s.has(1):
                        act.wait_ge(v_done, s.row(2))
                        wait(act, pv_done, s.row(-2) * H)
                        nc.scalar.activation(v_one[s.buf(1, 4)][:, :, :, 0:HD], bank_v[:, 0:QT * D].rearrange("p (t h d) -> p t h d", t=QT, h=H),
                                             ACT.Identity).then_inc(v_copied, 1)
                    exps(1)
                    if s.has(-3):
                        act.wait_ge(attT_done, s.row(-2))
                        wait(act, proj_done, s.row(-3))
                        nc.scalar.activation(attT[:], bank_T[:, 0:T], ACT.Identity).then_inc(attT_copied, 1)
                    exps(2)
                    exps(3)
                    if s.has(3):
                        act.wait_ge(zT_done, s.row(4))
                        wait(act, v_done, s.row(2))
                        nc.scalar.activation(zT[s.buf(3)][:], bank_T[:, 0:T], ACT.Identity, bias=one_col[:, 0:1]).then_inc(zT_copied, 1)

                all_slots(act, slot)

            @block.tensor
            def _(pe):
                pe.wait_ge(consts_set, 4)
                pe.wait_ge(w_gained, 4)
                nc.tensor.matmul(bank_kq[:, 0:3 * D], minus_mean[:], w_gain[:], start=True, stop=False)
                nc.tensor.matmul(bank_kq[:, 0:3 * D], b_mean[:], w_raw[:], start=False, stop=True).then_inc(w_mm, 1)
                pe.wait_ge(w_set, 1)

                def slot(pe, s):
                    def scores(h):
                        if s.has(0):
                            b = s.buf(0, 4)
                            if h == 0:
                                pe.wait_ge(packed_moved[b], (s.turn(0, 4) + 1) * (16 * PACK_DMAS))
                                pe.wait_ge(hi_packed, s.row(1))
                            wait(pe, row_max_set, s.row(0) * H + h)
                            for t in range(QT):
                                last = nc.tensor.matmul(bank_s[:, t * T:(t + 1) * T], packed[b][0:PARTS, h, QUERIES, t * P:(t + 1) * P],
                                                        packed[b][0:PARTS, h, KEYS, :], start=True, stop=True)
                            last.then_inc(s_done, 1)

                    def scoresT(u):
                        if s.has(-1):
                            b, pair, t = s.buf(-1, 4), u // QT, u % QT
                            pe.wait_ge(neg_max_set, s.row(0))
                            wait(pe, p_set, s.row(-1) * UNITS + (u - 1))
                            for i in range(2):
                                h = 2 * pair + i
                                last = nc.tensor.matmul(bank_sT[t][:, i * T:(i + 1) * T], packed[b][:, h, KEYS, t * P:(t + 1) * P],
                                                        packed[b][:, h, QUERIES, :], start=True, stop=True)
                            last.then_inc(sT_done, 1)

                    def weighted(h):
                        if s.has(-2):
                            pe.wait_ge(p_set, s.row(-2) * UNITS + (h // 2 + 1) * QT)
                            if h == 0:
                                wait(pe, att_set, s.row(-2))
                            heads = slice(FIRST_HEAD[h], FIRST_HEAD[h] + WIDE)
                            for q in range(QT):
                                for t in range(QT):
                                    last = nc.tensor.matmul(banks_o[:, q, h * O_COLS:(h + 1) * O_COLS], pT[s.buf(-2)][h // 2][:, t, h % 2, q * P:(q + 1) * P],
                                                            v_one[s.buf(-2, 4)][:, t, heads, :].rearrange("p h d -> p (h d)"),
                                                            start=(t == 0), stop=(t == QT - 1))
                            last.then_inc(pv_done, 1)

                    scores(0)
                    weighted(0)
                    scores(1)
                    weighted(1)
                    if s.has(2):
                        pe.wait_ge(zT_copied, s.row(3))
                        wait(pe, lo_split, s.row(2))
                        if s.has(-1):
                            pe.wait_ge(neg_max_set, s.row(0))
                        for i, cols in enumerate((slice(D, 2 * D), slice(0, D))):
                            last = nc.tensor.matmul(bank_kq[:, i * T:(i + 1) * T], w[:, cols], zT[s.buf(2)][:], start=True, stop=True)
                        last.then_inc(kq_done, 1)
                    scoresT(0)
                    if s.has(1):
                        pe.wait_ge(zT_copied, s.row(2))
                        wait(pe, y_set, s.row(-3))
                        for t in range(QT):
                            last = nc.tensor.matmul(bank_v[:, t * D:(t + 1) * D], zT[s.buf(1)][:, t * P:(t + 1) * P], w[:, 2 * D:3 * D], start=True, stop=True)
                        last.then_inc(v_done, 1)
                    scores(2)
                    weighted(2)
                    scoresT(1)
                    if s.has(-3):
                        pe.wait_ge(att_set, s.row(-2))
                        if s.has(2):
                            pe.wait_ge(zT_copied, s.row(3))
                        for t in range(QT):
                            last = nc.tensor.transpose(bank_T[:, t * P:(t + 1) * P], att[:, t, :, :].rearrange("p h d -> p (h d)"), ident[:])
                        last.then_inc(attT_done, 1)
                    scores(3)
                    weighted(3)
                    scoresT(2)
                    if s.has(-3):
                        pe.wait_ge(attT_copied, s.row(-2))
                        if s.has(1):
                            pe.wait_ge(v_copied, s.row(2))
                        elif s.has(-4):
                            pe.wait_ge(y_set, s.row(-3))
                        for t in range(QT):
                            last = nc.tensor.matmul(bank_v[:, t * D:(t + 1) * D], attT[:, t * P:(t + 1) * P], wp[:], start=True, stop=True)
                        last.then_inc(proj_done, 1)
                    if s.has(3):
                        pe.wait_ge(xn_set, s.row(4))
                        wait(pe, zT_copied, s.row(3))
                        wait(pe, attT_copied, s.row(-2))
                        for t in range(QT):
                            last = nc.tensor.transpose(bank_T[:, t * P:(t + 1) * P], xn[s.buf(3)][:, t, :], ident[:])
                        last.then_inc(zT_done, 1)
                    scoresT(3)
                    if s.has(0):
                        pe.wait_ge(max_split, s.row(1))
                        if s.has(2):
                            pe.wait_ge(lo_split, s.row(3))
                        for t in range(QT):
                            last = nc.tensor.matmul(bank_kq[:, t * P:(t + 1) * P], max_hl[s.buf(0)][:, t, :, :].rearrange("p h d -> p (h d)"), ident_bf[:],
                                                    start=True, stop=True)
                        last.then_inc(maxT_done, 1)

                all_slots(pe, slot)


def triangle_projections(nc, outgoing, x, ab, gate, ln_w, ln_b, w_parts, b_parts):
    L, T, D = x.shape
    JT = T // P
    CB = ab.shape[4]
    NCB = ab.shape[2]
    GI = 2
    SI = 16
    G = L // GI
    GS = SI // GI
    TILES = GI * JT
    assert D == P and NCB * CB == 2 * D and TILES * P == 512

    x_v = x.rearrange("(s i) (t p) c -> s p t i c", i=SI, p=P) if outgoing else x.rearrange("(t p) (s i) c -> s p t i c", i=SI, p=P)
    ab_v = ab.rearrange("t p n (s i) c -> s t p n (i c)", i=SI)
    gate_v = gate.rearrange("(t p) (s i) c -> s p t i c", i=SI, p=P)

    with ExitStack() as ctx:
        tag = "po_" if outgoing else "pi_"

        def sb(name, shape, dt=F32):
            return ctx.enter_context(nc.sbuf_tensor(tag + name, shape, dt))

        def bank(name):
            return ctx.enter_context(nc.psum_tensor(tag + name, [P, 512], F32))

        def sem(name):
            return ctx.enter_context(nc.semaphore(tag + name))

        NW = 5 * D
        ident, one_col = sb("ident", [P, P]), sb("one_col", [P, 1])
        half_neg, eps = sb("half_neg", [P, JT, GI]), sb("eps", [P, JT, GI])
        g_col, b_col, b_wide, minus_mean = sb("g_col", [P, 1]), sb("b_col", [P, 1]), sb("b_wide", [P, P]), sb("minus_mean", [P, P])
        b_mean = sb("b_mean", [P, P])
        w_raw, w_gain, bias, w_part, w = (sb(n, [P, NW]) for n in ("w_raw", "w_gain", "bias", "w_part", "w"))
        x_in = [sb(f"x_in{i}", [P, JT, SI, D]) for i in range(2)]
        ab_out = [sb(f"ab_out{i}", [P, JT, NCB, SI, CB]) for i in range(2)]
        gate_out = [sb(f"gate_out{i}", [P, JT, SI, D]) for i in range(2)]
        stats = [sb(f"stats{i}", [P, JT, GI, 6]) for i in range(2)]
        mean_var = [sb(f"mean_var{i}", [P, JT, GI, 2]) for i in range(2)]
        var_eps = [sb(f"var_eps{i}", [P, JT, GI]) for i in range(2)]
        rstd = [sb(f"rstd{i}", [P, JT, GI]) for i in range(2)]
        xn = [sb(f"xn{i}", [P, JT, GI, D]) for i in range(2)]
        zT = [sb(f"zT{i}", [P, TILES, P]) for i in range(2)]
        sig = [sb(f"sig{i}", [P, 2 * D]) for i in range(2)]
        bank_T = [bank(f"bank_T{i}") for i in range(2)]
        bank_ab = [bank(f"bank_ab{i}") for i in range(4)]
        bank_g = [bank(f"bank_g{i}") for i in range(2)]

        w_loaded, consts_set, w_gained, w_mm, w_set = (sem(n) for n in ("w_loaded", "consts_set", "w_gained", "w_mm", "w_set"))
        x_loaded, ab_stored, gate_stored = ([sem(f"{n}{i}") for i in range(2)] for n in ("x_loaded", "ab_stored", "gate_stored"))
        stats_set, mean_set, eps_set, rstd_set, xn_set, zT_done, zT_copied, ab_done, sig_set, ab_set, g_done, gate_set = (sem(n) for n in (
            "stats_set", "mean_set", "eps_set", "rstd_set", "xn_set", "zT_done", "zT_copied", "ab_done", "sig_set", "ab_set", "g_done", "gate_set"))

        LOADS = L // SI

        class Slot:

            def __init__(self, it, s0):
                self.it, self.s0, self.loop = it, s0, not isinstance(it, int)

            def has(self, k):
                return self.loop or 0 <= self.s0 + k < G

            def group(self, k):
                return self.it * (2 * GS) + (self.s0 + k)

            def turn(self, k):
                return self.it + (self.s0 + k) // (2 * GS)

            def buf(self, k):
                return (self.s0 + k) // GS % 2

            def pos(self, k):
                return (self.s0 + k) % GS

        def all_slots(slot):
            def run(engine):
                for s in range(-3, 0):
                    slot(Slot(0, s))
                with engine.Fori(0, LOADS // 2 - 1) as it:
                    for s in range(2 * GS):
                        slot(Slot(it, s))
                for s in range(G - 2 * GS, G):
                    slot(Slot(0, s))
            return run

        AB_AHEAD, GATE_AHEAD, G_DONE_AHEAD, STORED_AHEAD = TILES, 2, 1, 1

        with nc.Block() as block:

            @block.sync
            def _(sp):
                sp.dma_start(g_col[:], ln_w.rearrange("(c a) -> c a", a=1)).then_inc(w_loaded, 16)
                sp.dma_start(b_col[:], ln_b.rearrange("(c a) -> c a", a=1)).then_inc(w_loaded, 16)
                for i in range(5):
                    sp.dma_start(w_raw[:, i * D:(i + 1) * D], w_parts[i]).then_inc(w_loaded, 16)
                    sp.dma_start(bias[:, i * D:(i + 1) * D], b_parts[i].rearrange("(a c) -> a c", a=1).to_broadcast([P, D])).then_inc(w_loaded, 16)

                def load(n, buf):
                    for t in range(JT):
                        for half in (slice(0, SI // 2), slice(SI // 2, SI)):
                            sp.dma_start(x_in[buf][:, t, half, :], x_v[n, :, t, half]).then_inc(x_loaded[buf], 16)

                def store(n, buf):
                    sp.wait_ge(ab_set, (n + 1) * (GS * TILES) + AB_AHEAD)
                    for t in range(JT):
                        sp.dma_start(ab_v[n, t], ab_out[buf][:, t, :, :, :].rearrange("p n i c -> p n (i c)")).then_inc(ab_stored[buf], 16)
                    sp.wait_ge(gate_set, (n + 1) * GS + GATE_AHEAD)
                    for t in range(JT):
                        sp.dma_start(gate_v[n, :, t], gate_out[buf][:, t, :, :]).then_inc(gate_stored[buf], 16)

                for n in range(2):
                    load(n, n)
                with sp.Fori(0, LOADS // 2 - 1) as it:
                    for buf in range(2):
                        sp.wait_ge(xn_set, (it * 2 + (buf + 1)) * GS)
                        load(it * 2 + (buf + 2), buf)
                        store(it * 2 + buf, buf)
                for buf in range(2):
                    store(LOADS - 2 + buf, buf)
                for buf in range(2):
                    sp.wait_ge(ab_stored[buf], LOADS // 2 * JT * 16 + STORED_AHEAD)
                    sp.wait_ge(gate_stored[buf], LOADS // 2 * JT * 16 + STORED_AHEAD)

            @block.gpsimd
            def _(pool):
                nc.gpsimd.memset(minus_mean[:], -1.0 / D)
                nc.gpsimd.memset(one_col[:], 1.0)
                nc.gpsimd.memset(half_neg[:], -0.5)
                nc.gpsimd.memset(eps[:], EPS)
                nc.gpsimd.memset(ident[:], 0.0).then_inc(consts_set, 1)
                pool.wait_ge(consts_set, 1)
                nc.gpsimd.affine_select(out=ident[:], in_=ident[:], compare_op=ALU.not_equal, fill=1.0, base=0,
                                        pattern=[[-1, P]], channel_multiplier=1).then_inc(consts_set, 1)

                def slot(s):
                    if s.has(3):
                        b = s.pos(3) % 2
                        pool.wait_ge(mean_set, s.group(4))
                        nc.gpsimd.tensor_tensor(var_eps[b][:], mean_var[b][:, :, :, 1], eps[:], ALU.add).then_inc(eps_set, 1)
                        pool.wait_ge(eps_set, s.group(4))
                        nc.gpsimd.tensor_tensor(rstd[b][:], var_eps[b][:], half_neg[:], ALU.pow).then_inc(rstd_set, 1)

                all_slots(slot)(pool)

            @block.vector
            def _(dve):
                dve.sem_inc(ab_set, AB_AHEAD)
                for buf in range(2):
                    dve.sem_inc(ab_stored[buf], STORED_AHEAD)
                dve.wait_ge(w_loaded, 12 * 16)
                nc.vector.tensor_copy(b_wide[:], b_col[:, 0:1].to_broadcast([P, P])).then_inc(w_gained, 1)
                nc.vector.tensor_scalar(w_gain[:], w_raw[:], g_col[:, 0:1], None, ALU.mult).then_inc(w_gained, 1)
                dve.wait_ge(w_gained, 2)
                nc.vector.tensor_scalar(b_mean[:], b_wide[:], 1.0 / D, None, ALU.mult).then_inc(w_gained, 1)
                nc.vector.scalar_tensor_tensor(out=w_part[:], in0=bias[:], scalar=1.0 / D, in1=w_gain[:], op0=ALU.mult, op1=ALU.add).then_inc(w_gained, 1)
                dve.wait_ge(w_gained, 4)
                dve.wait_ge(w_mm, 1)
                nc.vector.tensor_tensor(w[:, 0:4 * D], bank_ab[0][:], w_part[:, 0:4 * D], ALU.add)
                nc.vector.tensor_tensor(w[:, 4 * D:NW], bank_ab[1][:, 0:D], w_part[:, 4 * D:NW], ALU.add).then_inc(w_set, 1)

                def slot(s):
                    def gated(tile):
                        dve.wait_ge(sig_set, s.group(0) * TILES + (tile + 1))
                        t, i = tile // GI, tile % GI
                        nc.vector.tensor_tensor(ab_out[s.buf(0)][:, t, :, s.pos(0) * GI + i, :],
                                                bank_ab[tile][:, 2 * D:4 * D].rearrange("p (n c) -> p n c", c=CB),
                                                sig[tile % 2][:].rearrange("p (n c) -> p n c", c=CB), ALU.mult).then_inc(ab_set, 1)

                    def normalise(t):
                        if s.has(2):
                            b = s.pos(2) % 2
                            if t == 0:
                                dve.wait_ge(rstd_set, s.group(3))
                                if s.has(0):
                                    dve.wait_ge(zT_done, s.group(1))
                            for i in range(GI):
                                last = nc.vector.tensor_scalar(xn[b][:, t, i, :], x_in[s.buf(2)][:, t, s.pos(2) * GI + i, :],
                                                               mean_var[b][:, t, i, 0:1], rstd[b][:, t, i:i + 1], ALU.subtract, ALU.mult)
                            if t == JT - 1:
                                last.then_inc(xn_set, 1)

                    if s.has(0):
                        if s.pos(0) == 0:
                            dve.wait_ge(ab_stored[s.buf(0)], s.turn(0) * (16 * JT) + STORED_AHEAD)
                        gated(0)
                    normalise(0)
                    if s.has(0):
                        gated(1)
                    normalise(1)
                    if s.has(3):
                        b = s.pos(3) % 2
                        if s.pos(3) == 0:
                            dve.wait_ge(x_loaded[s.buf(3)], (s.turn(3) + 1) * (2 * 16 * JT))
                        for t in range(JT):
                            for i in range(GI):
                                last = nc.vector.bn_stats(stats[b][:, t, i, :], x_in[s.buf(3)][:, t, s.pos(3) * GI + i, :])
                        last.then_inc(stats_set, 1)
                    if s.has(0):
                        gated(2)
                    if s.has(3):
                        dve.wait_ge(stats_set, s.group(4))
                    if s.has(0):
                        gated(3)
                    if s.has(3):
                        for t in range(JT):
                            for i in range(GI):
                                last = nc.vector.bn_aggr(mean_var[b][:, t, i, :], stats[b][:, t, i, :])
                        last.then_inc(mean_set, 1)

                all_slots(slot)(dve)

            @block.scalar
            def _(act):
                act.sem_inc(gate_set, GATE_AHEAD)
                for buf in range(2):
                    act.sem_inc(gate_stored[buf], STORED_AHEAD)
                act.wait_ge(consts_set, 1)

                def slot(s):
                    if s.has(1):
                        b = s.pos(1) % 2
                        act.wait_ge(zT_done, s.group(2))
                        if s.has(0):
                            act.wait_ge(g_done, s.group(0) + G_DONE_AHEAD)
                        nc.scalar.activation(zT[b][:].rearrange("p a b -> p (a b)"), bank_T[b][:], ACT.Identity, bias=one_col[:, 0:1]).then_inc(zT_copied, 1)
                    if s.has(0):
                        for tile in range(TILES):
                            act.wait_ge(ab_done, s.group(0) * TILES + (tile + 1))
                            act.wait_ge(ab_set, s.group(0) * TILES + (tile - 1 + AB_AHEAD))
                            nc.scalar.activation(sig[tile % 2][:], bank_ab[tile][:, 0:2 * D], ACT.Sigmoid).then_inc(sig_set, 1)
                        act.wait_ge(g_done, s.group(1) + G_DONE_AHEAD)
                        if s.pos(0) == 0:
                            act.wait_ge(gate_stored[s.buf(0)], s.turn(0) * (16 * JT) + STORED_AHEAD)
                        nc.scalar.activation(gate_out[s.buf(0)][:, :, s.pos(0) * GI:(s.pos(0) + 1) * GI, :],
                                             bank_g[s.pos(0) % 2][:].rearrange("p (t i c) -> p t i c", t=JT, i=GI), ACT.Sigmoid).then_inc(gate_set, 1)

                all_slots(slot)(act)

            @block.tensor
            def _(pe):
                pe.sem_inc(g_done, G_DONE_AHEAD)
                pe.wait_ge(consts_set, 2)
                pe.wait_ge(w_gained, 4)
                for bank_w, cols in ((bank_ab[0], slice(0, 4 * D)), (bank_ab[1], slice(4 * D, NW))):
                    out = bank_w[:, 0:cols.stop - cols.start]
                    nc.tensor.matmul(out, minus_mean[:], w_gain[:, cols], start=True, stop=False)
                    last = nc.tensor.matmul(out, b_mean[:], w_raw[:, cols], start=False, stop=True)
                last.then_inc(w_mm, 1)
                pe.wait_ge(w_set, 1)

                def slot(s):
                    if s.has(0):
                        pe.wait_ge(zT_copied, s.group(1))
                    if s.has(1):
                        b = s.pos(1) % 2
                        pe.wait_ge(xn_set, s.group(2))
                        for t in range(JT):
                            for i in range(GI):
                                last = nc.tensor.transpose(bank_T[b][:, (t * GI + i) * P:(t * GI + i + 1) * P], xn[b][:, t, i, :], ident[:])
                        last.then_inc(zT_done, 1)
                    if s.has(0):
                        b = s.pos(0) % 2
                        for tile in range(TILES):
                            pe.wait_ge(ab_set, s.group(0) * TILES + (tile + 1 - TILES + AB_AHEAD))
                            nc.tensor.matmul(bank_ab[tile][:], zT[b][:, tile, :], w[:, 0:4 * D], start=True, stop=True).then_inc(ab_done, 1)
                        pe.wait_ge(gate_set, s.group(0) + (GATE_AHEAD - 1))
                        for tile in range(TILES):
                            last = nc.tensor.matmul(bank_g[b][:, tile * D:(tile + 1) * D], zT[b][:, tile, :], w[:, 4 * D:NW], start=True, stop=True)
                        last.then_inc(g_done, 1)

                all_slots(slot)(pe)


def triangle_product(nc, outgoing, x, x_out, ab, gate, ln_w, ln_b, w_z, b_z):
    L, T, D = x.shape
    JT, _, NCB, _, CB = ab.shape
    NB = NCB // 2
    HALVES = L // P
    QUARTERS = HALVES * HALVES
    GK = 4
    EG = P // GK
    SLOTS = EG // NB * 2
    ITS = NB // 2
    PAIRS = SLOTS // 2
    BH = CB // 4
    assert SLOTS == 4 and BH == 2 and GK * P == 512

    ab_v = ab.rearrange("t p n i c -> n p t (i c)")
    x_v = x.rearrange("(h p) (f k) c -> h f p k c", p=P, k=2 * GK)
    out_v = x_out.rearrange("(h p) (f k) c -> h f p k c", p=P, k=2 * GK)
    gate_v = gate.rearrange("(f k) (h p) c -> h f p k c", p=P, k=2 * GK) if outgoing else gate.rearrange("(h p) (f k) c -> h f p k c", p=P, k=2 * GK)

    with ExitStack() as ctx:
        tag = "to_" if outgoing else "ti_"

        def sb(name, shape, dt=F32):
            return ctx.enter_context(nc.sbuf_tensor(tag + name, shape, dt))

        def bank(name):
            return ctx.enter_context(nc.psum_tensor(tag + name, [P, 512], F32))

        def sem(name):
            return ctx.enter_context(nc.semaphore(tag + name))

        ident, one_col = sb("ident", [P, P]), sb("one_col", [P, 1])
        half_neg, eps = sb("half_neg", [P, GK]), sb("eps", [P, GK])
        g_col, b_col = sb("g_col", [P, 1]), sb("b_col", [P, 1])
        w = sb("w", [P, D])
        a_in = [sb(f"a_in{i}", [P, JT, P, CB]) for i in range(2)]
        b_in = [sb(f"b_in{i}", [P, JT, P, CB]) for i in range(2)]
        p_acc = [sb(f"p_acc{i}", [P, P, D]) for i in range(2)]
        stats = [sb(f"stats{i}", [P, GK, 6]) for i in range(2)]
        mean_var = [sb(f"mean_var{i}", [P, GK, 2]) for i in range(2)]
        var_eps = [sb(f"var_eps{i}", [P, GK]) for i in range(2)]
        rstd = [sb(f"rstd{i}", [P, GK]) for i in range(2)]
        pn = [sb(f"pn{i}", [P, GK, D]) for i in range(2)]
        pT = [sb(f"pT{i}", [P, GK, P]) for i in range(2)]
        gated = [sb(f"gated{i}", [P, GK, D]) for i in range(2)]
        x_res = [sb(f"x_res{i}", [P, 2 * GK, D]) for i in range(2)]
        g_in = [sb(f"g_in{i}", [P, 2 * GK, D]) for i in range(2)]
        y = [sb(f"y{i}", [P, 2 * GK, D]) for i in range(2)]
        w_raw, w_gain, bias, w_part = (y[0][:, i, :] for i in range(4))
        b_wide, b_mean, minus_mean = (y[0][:, 4 + i, :] for i in range(3))
        bank_p = [bank(f"bank_p{i}") for i in range(2 * BH)]
        bank_T = [bank(f"bank_T{i}") for i in range(2)]
        bank_z = [bank(f"bank_z{i}") for i in range(2)]

        w_loaded, consts_set, w_gained, w_mm, w_set = (sem(n) for n in ("w_loaded", "consts_set", "w_gained", "w_mm", "w_set"))
        ab_loaded, xg_loaded, y_stored = ([sem(f"{n}{i}") for i in range(2)] for n in ("ab_loaded", "xg_loaded", "y_stored"))
        p_done, p_copied, stats_set, mean_set, eps_set, rstd_set, pn_set, pT_done, pT_copied, z_done, gated_set, y_set = (sem(n) for n in (
            "p_done", "p_copied", "stats_set", "mean_set", "eps_set", "rstd_set", "pn_set", "pT_done", "pT_copied", "z_done", "gated_set", "y_set"))

        P_AHEAD, GATED_AHEAD, Z_AHEAD, Y_AHEAD, STORED_AHEAD = 2 * BH, 2, 1, 2, 1

        class Slot:

            def __init__(self, quarter, it, j):
                self.quarter, self.it, self.j = quarter, it, j
                self.last = isinstance(it, int) and it == ITS - 1

            def group(self, k):
                return self.it * SLOTS + ((self.quarter - 1) * EG + self.j + k)

            def has(self, k):
                return not (self.quarter == QUARTERS and self.last and self.j + k >= SLOTS)

            def place(self, k):
                if self.last and self.j + k >= SLOTS:
                    return self.quarter % 2, (self.j + k - SLOTS) * GK
                return (self.quarter - 1) % 2, self.it * (SLOTS * GK) + (self.j + k) * GK

        def banks_of(it, j):
            if isinstance(it, int):
                return range(2 * j, 2 * j + 2) if j < SLOTS // 2 else ()
            return (j,)

        def steps(engine, slot, first):
            for quarter in range(first, QUARTERS + 1):
                with engine.Fori(0, ITS - 1) as it:
                    for j in range(SLOTS):
                        slot(quarter, it, j)
                for j in range(SLOTS):
                    slot(quarter, ITS - 1, j)
                yield quarter

        with nc.Block() as block:

            @block.sync
            def _(sp):
                sp.dma_start(g_col[:], ln_w.rearrange("(c a) -> c a", a=1)).then_inc(w_loaded, 16)
                sp.dma_start(b_col[:], ln_b.rearrange("(c a) -> c a", a=1)).then_inc(w_loaded, 16)
                sp.dma_start(w_raw, w_z).then_inc(w_loaded, 16)
                sp.dma_start(bias, b_z.rearrange("(a c) -> a c", a=1).to_broadcast([P, D])).then_inc(w_loaded, 16)

                def load_ab(quarter, block_at, buf):
                    ih, kh = quarter // HALVES, quarter % HALVES
                    n = P * CB
                    sp.dma_start(a_in[buf][:].rearrange("p t i c -> p t (i c)"), ab_v[block_at, :, :, ih * n:(ih + 1) * n]).then_inc(ab_loaded[buf], 16)
                    sp.dma_start(b_in[buf][:].rearrange("p t i c -> p t (i c)"), ab_v[block_at + NB, :, :, kh * n:(kh + 1) * n]).then_inc(ab_loaded[buf], 16)

                def load_xg(quarter, pair, buf):
                    ih, kh = quarter // HALVES, quarter % HALVES
                    sp.dma_start(x_res[buf][:], x_v[ih, pair + kh * (EG // 2)]).then_inc(xg_loaded[buf], 16)
                    sp.dma_start(g_in[buf][:], gate_v[ih, pair + kh * (EG // 2)]).then_inc(xg_loaded[buf], 16)

                for buf in range(2):
                    load_ab(0, buf, buf)
                    load_xg(0, buf, buf)

                def slot(quarter, it, j):
                    if j % 2:
                        return
                    buf = j // 2
                    last = isinstance(it, int) and it == ITS - 1
                    if quarter < QUARTERS and not (last and quarter == QUARTERS - 1):
                        sp.wait_ge(p_done, it * (2 * BH) + (quarter * NB + buf + 1) * BH)
                        if last:
                            load_ab(quarter + 1, buf, buf)
                        else:
                            load_ab(quarter, it * 2 + (buf + 2), buf)
                    if quarter > 0:
                        sp.wait_ge(y_set, it * SLOTS + ((quarter - 1) * EG + j + 2 + Y_AHEAD))
                        ih, kh = (quarter - 1) // HALVES, (quarter - 1) % HALVES
                        sp.dma_start(out_v[ih, it * PAIRS + (kh * (EG // 2) + buf)], y[buf][:]).then_inc(y_stored[buf], 16)
                        if not last:
                            load_xg(quarter - 1, it * PAIRS + (buf + 2), buf)
                        elif quarter < QUARTERS:
                            load_xg(quarter, buf, buf)

                for _ in steps(sp, slot, 0):
                    pass
                for buf in range(2):
                    sp.wait_ge(y_stored[buf], QUARTERS * ITS * 16 + STORED_AHEAD)

            @block.gpsimd
            def _(pool):
                pool.sem_inc(y_set, Y_AHEAD)
                for buf in range(2):
                    pool.sem_inc(y_stored[buf], STORED_AHEAD)
                nc.gpsimd.memset(minus_mean, -1.0 / D)
                nc.gpsimd.memset(one_col[:], 1.0)
                nc.gpsimd.memset(half_neg[:], -0.5)
                nc.gpsimd.memset(eps[:], EPS)
                nc.gpsimd.memset(ident[:], 0.0).then_inc(consts_set, 1)
                pool.wait_ge(consts_set, 1)
                nc.gpsimd.affine_select(out=ident[:], in_=ident[:], compare_op=ALU.not_equal, fill=1.0, base=0,
                                        pattern=[[-1, P]], channel_multiplier=1).then_inc(consts_set, 1)

                def power(b, count):
                    pool.wait_ge(mean_set, count)
                    nc.gpsimd.tensor_tensor(var_eps[b][:], mean_var[b][:, :, 1], eps[:], ALU.add).then_inc(eps_set, 1)
                    pool.wait_ge(eps_set, count)
                    nc.gpsimd.tensor_tensor(rstd[b][:], var_eps[b][:], half_neg[:], ALU.pow).then_inc(rstd_set, 1)

                for e in range(3):
                    power(e % 2, e + 1)
                pool.wait_ge(w_set, 1)

                def slot(quarter, it, j):
                    s = Slot(quarter, it, j)
                    if s.has(3):
                        power(1 - j % 2, s.group(4))
                    buf = j // 2
                    if j % 2 == 0:
                        turn = it + (quarter - 1) * ITS
                        pool.wait_ge(y_stored[buf], turn * 16 + STORED_AHEAD)
                        pool.wait_ge(xg_loaded[buf], (turn + 1) * 32)
                    pool.wait_ge(gated_set, s.group(1) + GATED_AHEAD)
                    cols = slice((j % 2) * GK, (j % 2 + 1) * GK)
                    nc.gpsimd.tensor_tensor(y[buf][:, cols, :], gated[j % 2][:], x_res[buf][:, cols, :], ALU.add).then_inc(y_set, 1)

                for _ in steps(pool, slot, 1):
                    pass

            @block.vector
            def _(dve):
                dve.sem_inc(gated_set, GATED_AHEAD)
                dve.wait_ge(w_loaded, 4 * 16)
                nc.vector.tensor_copy(b_wide, b_col[:, 0:1].to_broadcast([P, P])).then_inc(w_gained, 1)
                nc.vector.tensor_scalar(w_gain, w_raw, g_col[:, 0:1], None, ALU.mult).then_inc(w_gained, 1)
                dve.wait_ge(w_gained, 2)
                nc.vector.tensor_scalar(b_mean, b_wide, 1.0 / D, None, ALU.mult).then_inc(w_gained, 1)
                nc.vector.scalar_tensor_tensor(out=w_part, in0=bias, scalar=1.0 / D, in1=w_gain, op0=ALU.mult, op1=ALU.add).then_inc(w_gained, 1)
                dve.wait_ge(w_gained, 4)
                dve.wait_ge(w_mm, 1)
                nc.vector.tensor_tensor(w[:], bank_z[0][:, 0:D], w_part, ALU.add).then_inc(w_set, 1)

                def column(buf, k0, k):
                    at = k0 + k
                    return p_acc[buf][:, at, :] if isinstance(at, int) else p_acc[buf][:, bass.ds(at, 1), :].rearrange("p a c -> p (a c)")

                def statistics(b, place):
                    for k in range(GK):
                        last = nc.vector.bn_stats(stats[b][:, k, :], column(*place, k))
                    last.then_inc(stats_set, 1)

                def aggregate(b):
                    for k in range(GK):
                        last = nc.vector.bn_aggr(mean_var[b][:, k, :], stats[b][:, k, :])
                    last.then_inc(mean_set, 1)

                def normalise(b, place, count):
                    dve.wait_ge(rstd_set, count)
                    for k in range(GK):
                        last = nc.vector.tensor_scalar(pn[b][:, k, :], column(*place, k), mean_var[b][:, k, 0:1], rstd[b][:, k:k + 1],
                                                       ALU.subtract, ALU.mult)
                    last.then_inc(pn_set, 1)

                dve.wait_ge(p_copied, NB * BH + P_AHEAD)
                for e in range(3):
                    statistics(e % 2, (0, e * GK))
                    dve.wait_ge(stats_set, e + 1)
                    if e == 2:
                        normalise(0, (0, 0), 1)
                        dve.wait_ge(pn_set, 1)
                    aggregate(e % 2)

                def slot(quarter, it, j):
                    s = Slot(quarter, it, j)
                    b = j % 2
                    if s.has(1):
                        dve.wait_ge(pT_done, s.group(1))
                        normalise(1 - b, s.place(1), s.group(2))
                    if s.has(3):
                        if s.last and j + 3 == SLOTS:
                            dve.wait_ge(p_copied, (quarter + 1) * NB * BH + P_AHEAD)
                        statistics(1 - b, s.place(3))
                        dve.wait_ge(stats_set, s.group(4))
                    dve.wait_ge(z_done, s.group(1) + Z_AHEAD)
                    if j % 2 == 0:
                        dve.wait_ge(xg_loaded[j // 2], (it + ((quarter - 1) * ITS + 1)) * 32)
                    dve.wait_ge(y_set, s.group(-1) + Y_AHEAD)
                    cols = slice((j % 2) * GK, (j % 2 + 1) * GK)
                    nc.vector.tensor_tensor(gated[b][:].rearrange("p k c -> p (k c)"), bank_z[b][:], g_in[j // 2][:, cols, :].rearrange("p k c -> p (k c)"),
                                            ALU.mult).then_inc(gated_set, 1)
                    if s.has(3):
                        aggregate(1 - b)

                for _ in steps(dve, slot, 1):
                    pass

            @block.scalar
            def _(act):
                act.sem_inc(p_copied, P_AHEAD)
                act.wait_ge(consts_set, 1)

                def gather(quarter, it, j):
                    n = it * (2 * BH) + (quarter * NB * BH + j)
                    act.wait_ge(p_done, n + 1)
                    c0 = (j // BH) * CB + (j % BH) * 4 + it * (2 * CB)
                    cols = slice(c0, c0 + 4) if isinstance(c0, int) else bass.ds(c0, 4)
                    nc.scalar.activation(p_acc[quarter % 2][:, :, cols].rearrange("p k c -> p c k"), bank_p[j][:].rearrange("p (c k) -> p c k", c=4),
                                         ACT.Identity).then_inc(p_copied, 1)

                def copy(b, count):
                    act.wait_ge(pT_done, count)
                    nc.scalar.activation(pT[b][:].rearrange("p a b -> p (a b)"), bank_T[b][:], ACT.Identity, bias=one_col[:, 0:1]).then_inc(pT_copied, 1)

                def slot(quarter, it, j):
                    if quarter < QUARTERS:
                        for j_bank in banks_of(it, j):
                            gather(quarter, it, j_bank)
                    if quarter > 0:
                        s = Slot(quarter, it, j)
                        if s.has(1):
                            act.wait_ge(z_done, s.group(0) + Z_AHEAD)
                            copy(1 - j % 2, s.group(2))

                for quarter in steps(act, slot, 0):
                    if quarter == 0:
                        copy(0, 1)

            @block.tensor
            def _(pe):
                pe.sem_inc(z_done, Z_AHEAD)
                pe.wait_ge(consts_set, 2)
                pe.wait_ge(w_gained, 4)
                nc.tensor.matmul(bank_z[0][:, 0:D], minus_mean, w_gain, start=True, stop=False)
                nc.tensor.matmul(bank_z[0][:, 0:D], b_mean, w_raw, start=False, stop=True).then_inc(w_mm, 1)
                pe.wait_ge(w_set, 1)

                def products(quarter, it, j):
                    buf, half = j // BH, j % BH
                    if half == 0:
                        pe.wait_ge(ab_loaded[buf], (it + (quarter * ITS + 1)) * 32)
                    pe.wait_ge(p_copied, it * (2 * BH) + (quarter * NB * BH + j + 1 - 2 * BH + P_AHEAD))
                    for c in range(4):
                        for t in range(JT):
                            last = nc.tensor.matmul(bank_p[j][:, c * P:(c + 1) * P], a_in[buf][:, t, :, half * 4 + c], b_in[buf][:, t, :, half * 4 + c],
                                                    start=(t == 0), stop=(t == JT - 1))
                    last.then_inc(p_done, 1)

                def turn(b, count):
                    pe.wait_ge(pn_set, count)
                    for k in range(GK):
                        last = nc.tensor.transpose(bank_T[b][:, k * P:(k + 1) * P], pn[b][:, k, :], ident[:])
                    last.then_inc(pT_done, 1)

                def slot(quarter, it, j):
                    if quarter < QUARTERS:
                        for j_bank in banks_of(it, j):
                            products(quarter, it, j_bank)
                    if quarter > 0:
                        s = Slot(quarter, it, j)
                        b = j % 2
                        pe.wait_ge(pT_copied, s.group(1))
                        pe.wait_ge(gated_set, s.group(-1) + GATED_AHEAD)
                        for k in range(GK):
                            last = nc.tensor.matmul(bank_z[b][:, k * D:(k + 1) * D], pT[b][:, k, :], w[:], start=True, stop=True)
                        last.then_inc(z_done, 1)
                        if s.has(1):
                            turn(1 - b, s.group(2))

                for quarter in steps(pe, slot, 0):
                    if quarter == 0:
                        turn(0, 1)


def pair_stack(nc, out, x, at_ln_g, at_ln_b, w_qkv, b_qkv, w_proj, b_proj, ln_in_w, ln_in_b, w_ag, b_ag, w_ap, b_ap,
               w_bg, b_bg, w_bp, b_bp, ln_out_w, ln_out_b, w_z, b_z, w_g, b_g):
    x, out = x[0], out[0]
    L, _, D = x.shape
    CB = 8
    x_at = nc.dram_tensor("x_at", (L, L, D), F32, kind="Internal").ap()
    x_mid = nc.dram_tensor("x_mid", (L, L, D), F32, kind="Internal").ap()
    ab = nc.dram_tensor("ab", (L // P, P, 2 * D // CB, L, CB), F32, kind="Internal").ap()
    gate = nc.dram_tensor("gate", (L, L, D), F32, kind="Internal").ap()

    attention_layer(nc, x, x_at, at_ln_g, at_ln_b, w_qkv, b_qkv, w_proj, b_proj)
    for idx, (outgoing, src, dst) in enumerate(((True, x_at, x_mid), (False, x_mid, out))):
        nc.all_engine_barrier()
        triangle_projections(nc, outgoing, src, ab, gate, ln_in_w[idx], ln_in_b[idx],
                             [m[idx] for m in (w_ag, w_bg, w_ap, w_bp, w_g)], [m[idx] for m in (b_ag, b_bg, b_ap, b_bp, b_g)])
        nc.all_engine_barrier()
        triangle_product(nc, outgoing, src, dst, ab, gate, ln_out_w[idx], ln_out_b[idx], w_z[idx], b_z[idx])


_INS = ["x", "L0_conv_ln_g", "L0_conv_ln_b", "L0_conv_w_qkv", "L0_conv_b_qkv", "L0_conv_w_proj", "L0_conv_b_proj",
        "L1_conv_ln_in_w", "L1_conv_ln_in_b", "L1_conv_w_ag", "L1_conv_b_ag", "L1_conv_w_ap", "L1_conv_b_ap",
        "L1_conv_w_bg", "L1_conv_b_bg", "L1_conv_w_bp", "L1_conv_b_bp", "L1_conv_ln_out_w", "L1_conv_ln_out_b",
        "L1_conv_w_z", "L1_conv_b_z", "L1_conv_w_g", "L1_conv_b_g"]


def kernel(**inputs):
    import numpy as np
    import concourse.bacc as bacc
    from concourse.bass_utils import run_bass_kernel_spmd

    nc = bacc.Bacc("TRN2", target_bir_lowering=False, num_devices=1)
    arrays = {f"in_{name}": np.ascontiguousarray(inputs[name]) for name in _INS}
    ins = [nc.dram_tensor(name, a.shape, mybir.dt.from_np(a.dtype), kind="ExternalInput").ap() for name, a in arrays.items()]
    out = nc.dram_tensor("out", arrays["in_x"].shape, F32, kind="ExternalOutput").ap()
    pair_stack(nc, out, *ins)
    return run_bass_kernel_spmd(nc, [arrays], core_ids=[0]).results[0]["out"]
```

```python
import math
from contextlib import ExitStack

import concourse.bass as bass
from concourse import mybir

P = 128
EPS = 1e-5

ALU = mybir.AluOpType
ACT = mybir.ActivationFunctionType
F32 = mybir.dt.float32
F32R = mybir.dt.float32r
BF16 = mybir.dt.bfloat16
AX_X = mybir.AxisListType.X




def attention_layer(nc, x, x_out, ln_g, ln_b, w_qkv, b_qkv, w_proj, b_proj):
    L, T, D = x.shape
    H, HD = 4, D // 4
    QT = T // P
    UNITS = QT * H // 2
    SCALE = 1.0 / math.sqrt(HD)
    assert D == P and QT == 2 and L % 2 == 0

    x_v = x.rearrange("r (p t) c -> r p t c", t=QT)
    out_v = x_out.rearrange("r (p t) c -> r p t c", t=QT)

    with ExitStack() as ctx:
        def sb(name, shape, dt=F32):
            return ctx.enter_context(nc.sbuf_tensor("at_" + name, shape, dt))

        def bank(name):
            return ctx.enter_context(nc.psum_tensor("at_" + name, [P, 512], F32))

        def sem(name):
            return ctx.enter_context(nc.semaphore("at_" + name))

        ident, one_col = sb("ident", [P, P]), sb("one_col", [P, 1])
        ident_bf = sb("ident_bf", [P, P], BF16)
        half_neg, eps = sb("half_neg", [P, QT]), sb("eps", [P, QT])
        g_col, b_col, b_wide = sb("g_col", [P, 1]), sb("b_col", [P, 1]), sb("b_wide", [P, P])
        minus_mean, b_mean = sb("minus_mean", [P, P]), sb("b_mean", [P, P])
        w_raw, w_gain, bias, w_part, w = (sb(n, [P, 3 * D]) for n in ("w_raw", "w_gain", "bias", "w_part", "w"))
        wp, proj_bias = sb("wp", [P, D]), sb("proj_bias", [P, D])
        x_in = [sb(f"x_in{i}", [P, QT, D]) for i in range(2)]
        stats = [sb(f"stats{i}", [P, QT, 6]) for i in range(2)]
        mean_var = [sb(f"mean_var{i}", [P, QT, 2]) for i in range(2)]
        var_eps = [sb(f"var_eps{i}", [P, QT]) for i in range(2)]
        rstd = [sb(f"rstd{i}", [P, QT]) for i in range(2)]
        xn = [sb(f"xn{i}", [P, QT, D]) for i in range(2)]
        zT = [sb(f"zT{i}", [P, T]) for i in range(2)]
        K_LO, K_HI, Q_HI, Q_LO = range(4)
        parts = [sb(f"parts{i}", [P, 4, T], F32R) for i in range(2)]
        KEYS, QUERIES = range(2)
        PARTS, MAX_ROWS = 3 * HD, slice(3 * HD, 4 * HD)
        packed = [sb(f"packed{i}", [P, H, 2, T], F32R) for i in range(4)]
        PACK_DMAS = 2 * H
        v_one = [sb(f"v_one{i}", [P, QT, H, HD + 1]) for i in range(4)]
        row_max = [sb(f"row_max{i}", [P, QT, H]) for i in range(2)]
        max_hl = [sb(f"max_hl{i}", [P, QT, H, HD], BF16) for i in range(2)]
        x_res = [sb(f"x_res{i}", [P, QT, D]) for i in range(2)]
        x_bias = [sb(f"x_bias{i}", [P, QT, D]) for i in range(2)]
        y = [sb(f"y{i}", [P, QT, D]) for i in range(2)]
        pT = [[sb(f"pT{i}{pair}", [P, QT, 2, T]) for pair in range(H // 2)] for i in range(2)]
        recip = sb("recip", [P, QT, H])
        att = sb("att", [P, QT, H, HD])
        attT = sb("attT", [P, T])

        bank_T, bank_kq, bank_v, bank_s = bank("bank_T"), bank("bank_kq"), bank("bank_v"), bank("bank_s")
        bank_sT = [bank(f"bank_sT{i}") for i in range(2)]
        banks_o = ctx.enter_context(nc.psum_tensor("at_banks_o", [P, QT, 512], F32))
        WIDE = H - 1
        FIRST_HEAD = [h // 2 for h in range(H)]
        O_COLS = WIDE * (HD + 1)
        O_OWN = [h * O_COLS + (h - FIRST_HEAD[h]) * (HD + 1) for h in range(H)]

        def own_sums(pair):
            step = O_OWN[2 * pair + 1] - O_OWN[2 * pair]
            return banks_o[:, :, O_OWN[2 * pair]:O_OWN[2 * pair] + 2 * step].rearrange("p t (h d) -> p t h d", h=2)

        w_loaded, consts_set, w_gained, w_mm, w_set = (sem(n) for n in ("w_loaded", "consts_set", "w_gained", "w_mm", "w_set"))
        x_loaded, res_loaded, y_stored = ([sem(f"{n}{i}") for i in range(2)] for n in ("x_loaded", "res_loaded", "y_stored"))
        packed_moved = [sem(f"packed_moved{i}") for i in range(4)]
        (stats_set, mean_set, eps_set, rstd_set, xn_set, zT_done, zT_copied, kq_done, hi_split, lo_split, hi_packed, v_done, v_copied,
         s_done, row_max_set, max_hi_set, max_split, maxT_done, neg_max_set, sT_done, p_set, pv_done, recip_set,
         att_set, attT_done, attT_copied, proj_done, x_bias_set, y_set) = (sem(n) for n in (
            "stats_set", "mean_set", "eps_set", "rstd_set", "xn_set", "zT_done", "zT_copied", "kq_done", "hi_split", "lo_split", "hi_packed",
            "v_done", "v_copied", "s_done", "row_max_set", "max_hi_set", "max_split", "maxT_done", "neg_max_set", "sT_done", "p_set", "pv_done",
            "recip_set", "att_set", "attT_done", "attT_copied", "proj_done", "x_bias_set", "y_set"))

        class Slot:

            def __init__(self, it, s0):
                self.it, self.s0, self.loop = it, s0, not isinstance(it, int)

            def has(self, k):
                return self.loop or 0 <= self.s0 + k < L

            def row(self, k):
                return self.it * 4 + (self.s0 + k)

            def turn(self, k, ring=2):
                return self.it * (4 // ring) + (self.s0 + k) // ring

            def buf(self, k, ring=2):
                return (self.s0 + k) % ring

        AHEAD, BEHIND, LOOP_FROM = 5, 4, 8

        def all_slots(engine, slot):
            for s in range(-AHEAD, LOOP_FROM):
                slot(engine, Slot(0, s))
            n = (L - AHEAD - LOOP_FROM) // 4
            with engine.Fori(0, n) as it:
                for j in range(4):
                    slot(engine, Slot(it, LOOP_FROM + j))
            for s in range(LOOP_FROM + 4 * n, L + BEHIND):
                slot(engine, Slot(0, s))

        def wait(engine, s, value):
            if not isinstance(value, int) or value > 0:
                engine.wait_ge(s, value)

        with nc.Block() as block:

            @block.sync
            def _(sp):
                sp.dma_start(g_col[:], ln_g.rearrange("(c a) -> c a", a=1)).then_inc(w_loaded, 16)
                sp.dma_start(b_col[:], ln_b.rearrange("(c a) -> c a", a=1)).then_inc(w_loaded, 16)
                sp.dma_start(w_raw[:], w_qkv).then_inc(w_loaded, 16)
                sp.dma_start(wp[:], w_proj).then_inc(w_loaded, 16)
                sp.dma_start(bias[:], b_qkv.rearrange("(a c) -> a c", a=1).to_broadcast([P, 3 * D])).then_inc(w_loaded, 16)
                sp.dma_start(proj_bias[:], b_proj.rearrange("(a c) -> a c", a=1).to_broadcast([P, D])).then_inc(w_loaded, 16)

                def slot(sp, s):
                    if s.has(-4):
                        sp.wait_ge(y_set, s.row(-3))
                        sp.dma_start(out_v[s.row(-4)], y[s.buf(-4)][:]).then_inc(y_stored[s.buf(-4)], 16)
                    if s.has(2):
                        b, to = s.buf(2), s.buf(2, 4)
                        sp.wait_ge(lo_split, s.row(3))
                        wait(sp, sT_done, s.row(-1) * UNITS)
                        for h in range(H):
                            for block, first in ((1, K_LO), (2, K_HI)):
                                sp.dma_start(packed[to][HD * block:HD * (block + 1), h, :, :].bitcast(F32),
                                             parts[b][HD * h:HD * (h + 1), first:first + 3:2, :].bitcast(F32)).then_inc(packed_moved[to], 16)
                    if s.has(5):
                        wait(sp, xn_set, s.row(4))
                        sp.dma_start(x_in[s.buf(5)][:], x_v[s.row(5)]).then_inc(x_loaded[s.buf(5)], 16)
                    if s.has(-2):
                        wait(sp, x_bias_set, s.row(-3))
                        sp.dma_start(x_res[s.buf(-2)][:], x_v[s.row(-2)]).then_inc(res_loaded[s.buf(-2)], 16)

                all_slots(sp, slot)
                for i in range(2):
                    sp.wait_ge(y_stored[i], 16 * (L // 2))

            @block.gpsimd
            def _(pool):
                nc.gpsimd.memset(minus_mean[:], -1.0 / D)
                nc.gpsimd.memset(one_col[:], 1.0)
                nc.gpsimd.memset(ident[:], 0.0)
                nc.gpsimd.memset(half_neg[:], -0.5)
                nc.gpsimd.memset(eps[:], EPS)
                for i in range(4):
                    nc.gpsimd.memset(v_one[i][:], 1.0)
                for i in range(2):
                    nc.gpsimd.memset(max_hl[i][:], 0.0)
                nc.gpsimd.memset(ident_bf[:], 0.0).then_inc(consts_set, 1)
                pool.wait_ge(consts_set, 1)
                for i in range(4):
                    last = nc.gpsimd.memset(packed[i][MAX_ROWS].bitcast(F32), 0.0)
                last.then_inc(consts_set, 1)
                pool.wait_ge(consts_set, 2)
                for i in range(4):
                    last = nc.gpsimd.memset(packed[i][PARTS:PARTS + 2, :, KEYS, :].bitcast(F32), 1.0)
                last.then_inc(consts_set, 1)
                pool.wait_ge(consts_set, 3)
                nc.gpsimd.affine_select(out=ident[:], in_=ident[:], compare_op=ALU.not_equal, fill=1.0, base=0,
                                        pattern=[[-1, P]], channel_multiplier=1)
                nc.gpsimd.affine_select(out=ident_bf[:], in_=ident_bf[:], compare_op=ALU.not_equal, fill=1.0, base=0,
                                        pattern=[[-1, P]], channel_multiplier=1).then_inc(consts_set, 1)

                def slot(pool, s):
                    if s.has(-3):
                        b = s.buf(-3)
                        pool.wait_ge(res_loaded[b], (s.turn(-3) + 1) * 16)
                        wait(pool, y_set, s.row(-4))
                        nc.gpsimd.tensor_tensor(x_bias[b][:], x_res[b][:], proj_bias[:].rearrange("p (a c) -> p a c", a=1).to_broadcast([P, QT, D]),
                                                ALU.add).then_inc(x_bias_set, 1)
                    if s.has(4):
                        b = s.buf(4)
                        pool.wait_ge(mean_set, s.row(5))
                        nc.gpsimd.tensor_tensor(var_eps[b][:], mean_var[b][:, :, 1], eps[:], ALU.add).then_inc(eps_set, 1)
                        pool.wait_ge(eps_set, s.row(5))
                        nc.gpsimd.tensor_tensor(rstd[b][:], var_eps[b][:], half_neg[:], ALU.pow).then_inc(rstd_set, 1)

                pool.wait_ge(w_loaded, 6 * 16)
                all_slots(pool, slot)

            @block.vector
            def _(dve):
                dve.wait_ge(w_loaded, 6 * 16)
                nc.vector.tensor_copy(b_wide[:], b_col[:, 0:1].to_broadcast([P, P])).then_inc(w_gained, 1)
                nc.vector.tensor_scalar(w_gain[:], w_raw[:], g_col[:, 0:1], None, ALU.mult).then_inc(w_gained, 1)
                dve.wait_ge(w_gained, 2)
                nc.vector.tensor_scalar(b_mean[:], b_wide[:], 1.0 / D, None, ALU.mult).then_inc(w_gained, 1)
                nc.vector.scalar_tensor_tensor(out=w_part[:], in0=bias[:], scalar=1.0 / D, in1=w_gain[:], op0=ALU.mult, op1=ALU.add).then_inc(w_gained, 1)
                dve.wait_ge(w_gained, 4)
                dve.wait_ge(w_mm, 1)
                nc.vector.tensor_tensor(w[:], bank_kq[:, 0:3 * D], w_part[:], ALU.add).then_inc(w_set, 1)
                dve.wait_ge(consts_set, 1)

                def slot(dve, s):
                    def maximum(h):
                        if s.has(0):
                            dve.wait_ge(s_done, s.row(0) * H + (h + 1))
                            nc.vector.tensor_reduce(row_max[s.buf(0)][:, :, h], bank_s[:].rearrange("p (t k) -> p t k", t=QT),
                                                    AX_X, ALU.max).then_inc(row_max_set, 1)

                    maximum(0)
                    if s.has(-4):
                        b = s.buf(-4)
                        dve.wait_ge(proj_done, s.row(-3))
                        dve.wait_ge(x_bias_set, s.row(-3))
                        wait(dve, y_stored[b], s.turn(-4) * 16)
                        nc.vector.tensor_tensor(y[b][:], bank_v[:, 0:QT * D].rearrange("p (t c) -> p t c", t=QT), x_bias[b][:],
                                                ALU.add).then_inc(y_set, 1)
                    if s.has(3):
                        b = s.buf(3)
                        dve.wait_ge(rstd_set, s.row(4))
                        wait(dve, zT_done, s.row(2))
                        for t in range(QT):
                            last = nc.vector.tensor_scalar(xn[b][:, t, :], x_in[b][:, t, :], mean_var[b][:, t, 0:1], rstd[b][:, t:t + 1],
                                                           ALU.subtract, ALU.mult)
                        last.then_inc(xn_set, 1)
                    maximum(1)
                    maximum(2)
                    if s.has(2):
                        b = s.buf(2)
                        dve.wait_ge(hi_split, s.row(3))
                        if s.has(0):
                            dve.wait_ge(packed_moved[s.buf(0, 4)], (s.turn(0, 4) + 1) * (16 * PACK_DMAS))
                        nc.vector.tensor_tensor(parts[b][:, K_LO:Q_LO + 1:3, :], bank_kq[:].rearrange("p (a t) -> p a t", a=2),
                                                parts[b][:, K_HI:Q_HI + 1, :].bitcast(F32), ALU.subtract).then_inc(lo_split, 1)
                    if s.has(4):
                        b = s.buf(4)
                        dve.wait_ge(x_loaded[b], (s.turn(4) + 1) * 16)
                        for t in range(QT):
                            last = nc.vector.bn_stats(stats[b][:, t, :], x_in[b][:, t, :])
                        last.then_inc(stats_set, 1)
                        dve.wait_ge(stats_set, s.row(5))
                    maximum(3)
                    if s.has(-2):
                        dve.wait_ge(pv_done, s.row(-1) * H)
                        for pair in range(H // 2):
                            last = nc.vector.reciprocal(recip[:, :, 2 * pair:2 * pair + 2], own_sums(pair)[:, :, :, HD])
                        last.then_inc(recip_set, 1)
                    if s.has(0):
                        b = s.buf(0)
                        dve.wait_ge(row_max_set, s.row(1) * H)
                        nc.vector.tensor_copy(max_hl[b][:, :, :, 0], row_max[b][:]).then_inc(max_hi_set, 1)
                    if s.has(-2):
                        dve.wait_ge(recip_set, s.row(-1))
                        wait(dve, attT_done, s.row(-2))
                        for pair in range(H // 2):
                            last = nc.vector.tensor_tensor(att[:, :, 2 * pair:2 * pair + 2, :], own_sums(pair)[:, :, :, 0:HD],
                                                           recip[:, :, 2 * pair:2 * pair + 2].rearrange("p t (h d) -> p t h d", d=1).to_broadcast([P, QT, 2, HD]),
                                                           ALU.mult)
                        last.then_inc(att_set, 1)
                    if s.has(0):
                        b = s.buf(0)
                        dve.wait_ge(max_hi_set, s.row(1))
                        nc.vector.tensor_tensor(max_hl[b][:, :, :, 1], row_max[b][:], max_hl[b][:, :, :, 0], ALU.subtract).then_inc(max_split, 1)
                    if s.has(4):
                        b = s.buf(4)
                        for t in range(QT):
                            last = nc.vector.bn_aggr(mean_var[b][:, t, :], stats[b][:, t, :])
                        last.then_inc(mean_set, 1)

                all_slots(dve, slot)

            @block.scalar
            def _(act):
                act.wait_ge(consts_set, 4)

                def slot(act, s):
                    def exps(u):
                        if s.has(-1):
                            pair, t = u // QT, u % QT
                            act.wait_ge(sT_done, s.row(-1) * UNITS + (u + 1))
                            wait(act, pv_done, s.row(-2) * H)
                            nc.scalar.activation(pT[s.buf(-1)][pair][:, t, :, :].rearrange("p h q -> p (h q)"), bank_sT[t][:], ACT.Exp,
                                                 scale=SCALE).then_inc(p_set, 1)

                    if s.has(-1):
                        act.wait_ge(maxT_done, s.row(0))
                        for h in range(H):
                            last = nc.scalar.activation(packed[s.buf(-1, 4)][MAX_ROWS, h, QUERIES, :], bank_kq[HD * h:HD * (h + 1), 0:T], ACT.Copy, scale=-1.0)
                        last.then_inc(neg_max_set, 1)
                    if s.has(1):
                        act.wait_ge(hi_split, s.row(2))
                        wait(act, sT_done, s.row(-2) * UNITS)
                        for h in range(H):
                            last = nc.scalar.activation(packed[s.buf(1, 4)][0:HD, h, :, :].rearrange("p a t -> p (a t)"),
                                                        parts[s.buf(1)][HD * h:HD * (h + 1), K_HI:Q_HI + 1, :].bitcast(F32).rearrange("p a t -> p (a t)"), ACT.Identity)
                        last.then_inc(hi_packed, 1)
                    if s.has(2):
                        act.wait_ge(kq_done, s.row(3))
                        wait(act, hi_packed, s.row(1))
                        if s.has(0):
                            act.wait_ge(packed_moved[s.buf(0, 4)], (s.turn(0, 4) + 1) * (16 * PACK_DMAS))
                        nc.scalar.activation(parts[s.buf(2)][:, K_HI:Q_HI + 1, :].rearrange("p a t -> p (a t)"), bank_kq[:], ACT.Identity).then_inc(hi_split, 1)
                    exps(0)
                    if s.has(1):
                        act.wait_ge(v_done, s.row(2))
                        wait(act, pv_done, s.row(-2) * H)
                        nc.scalar.activation(v_one[s.buf(1, 4)][:, :, :, 0:HD], bank_v[:, 0:QT * D].rearrange("p (t h d) -> p t h d", t=QT, h=H),
                                             ACT.Identity).then_inc(v_copied, 1)
                    exps(1)
                    if s.has(-3):
                        act.wait_ge(attT_done, s.row(-2))
                        wait(act, proj_done, s.row(-3))
                        nc.scalar.activation(attT[:], bank_T[:, 0:T], ACT.Identity).then_inc(attT_copied, 1)
                    exps(2)
                    exps(3)
                    if s.has(3):
                        act.wait_ge(zT_done, s.row(4))
                        wait(act, v_done, s.row(2))
                        nc.scalar.activation(zT[s.buf(3)][:], bank_T[:, 0:T], ACT.Identity, bias=one_col[:, 0:1]).then_inc(zT_copied, 1)

                all_slots(act, slot)

            @block.tensor
            def _(pe):
                pe.wait_ge(consts_set, 4)
                pe.wait_ge(w_gained, 4)
                nc.tensor.matmul(bank_kq[:, 0:3 * D], minus_mean[:], w_gain[:], start=True, stop=False)
                nc.tensor.matmul(bank_kq[:, 0:3 * D], b_mean[:], w_raw[:], start=False, stop=True).then_inc(w_mm, 1)
                pe.wait_ge(w_set, 1)

                def slot(pe, s):
                    def scores(h):
                        if s.has(0):
                            b = s.buf(0, 4)
                            if h == 0:
                                pe.wait_ge(packed_moved[b], (s.turn(0, 4) + 1) * (16 * PACK_DMAS))
                                pe.wait_ge(hi_packed, s.row(1))
                            wait(pe, row_max_set, s.row(0) * H + h)
                            for t in range(QT):
                                last = nc.tensor.matmul(bank_s[:, t * T:(t + 1) * T], packed[b][0:PARTS, h, QUERIES, t * P:(t + 1) * P],
                                                        packed[b][0:PARTS, h, KEYS, :], start=True, stop=True)
                            last.then_inc(s_done, 1)

                    def scoresT(u):
                        if s.has(-1):
                            b, pair, t = s.buf(-1, 4), u // QT, u % QT
                            pe.wait_ge(neg_max_set, s.row(0))
                            wait(pe, p_set, s.row(-1) * UNITS + (u - 1))
                            for i in range(2):
                                h = 2 * pair + i
                                last = nc.tensor.matmul(bank_sT[t][:, i * T:(i + 1) * T], packed[b][:, h, KEYS, t * P:(t + 1) * P],
                                                        packed[b][:, h, QUERIES, :], start=True, stop=True)
                            last.then_inc(sT_done, 1)

                    def weighted(h):
                        if s.has(-2):
                            pe.wait_ge(p_set, s.row(-2) * UNITS + (h // 2 + 1) * QT)
                            if h == 0:
                                wait(pe, att_set, s.row(-2))
                            heads = slice(FIRST_HEAD[h], FIRST_HEAD[h] + WIDE)
                            for q in range(QT):
                                for t in range(QT):
                                    last = nc.tensor.matmul(banks_o[:, q, h * O_COLS:(h + 1) * O_COLS], pT[s.buf(-2)][h // 2][:, t, h % 2, q * P:(q + 1) * P],
                                                            v_one[s.buf(-2, 4)][:, t, heads, :].rearrange("p h d -> p (h d)"),
                                                            start=(t == 0), stop=(t == QT - 1))
                            last.then_inc(pv_done, 1)

                    scores(0)
                    if s.has(-1):
                        pe.wait_ge(max_split, s.row(0))
                        if s.has(1):
                            pe.wait_ge(lo_split, s.row(2))
                        for t in range(QT):
                            last = nc.tensor.matmul(bank_kq[:, t * P:(t + 1) * P], max_hl[s.buf(-1)][:, t, :, :].rearrange("p h d -> p (h d)"), ident_bf[:],
                                                    start=True, stop=True)
                        last.then_inc(maxT_done, 1)
                    weighted(0)
                    scores(1)
                    weighted(1)
                    if s.has(2):
                        pe.wait_ge(zT_copied, s.row(3))
                        wait(pe, lo_split, s.row(2))
                        if s.has(-1):
                            pe.wait_ge(neg_max_set, s.row(0))
                        for i, cols in enumerate((slice(D, 2 * D), slice(0, D))):
                            last = nc.tensor.matmul(bank_kq[:, i * T:(i + 1) * T], w[:, cols], zT[s.buf(2)][:], start=True, stop=True)
                        last.then_inc(kq_done, 1)
                    scoresT(0)
                    if s.has(1):
                        pe.wait_ge(zT_copied, s.row(2))
                        wait(pe, y_set, s.row(-3))
                        for t in range(QT):
                            last = nc.tensor.matmul(bank_v[:, t * D:(t + 1) * D], zT[s.buf(1)][:, t * P:(t + 1) * P], w[:, 2 * D:3 * D], start=True, stop=True)
                        last.then_inc(v_done, 1)
                    scores(2)
                    weighted(2)
                    scoresT(1)
                    if s.has(-3):
                        pe.wait_ge(att_set, s.row(-2))
                        if s.has(2):
                            pe.wait_ge(zT_copied, s.row(3))
                        for t in range(QT):
                            last = nc.tensor.transpose(bank_T[:, t * P:(t + 1) * P], att[:, t, :, :].rearrange("p h d -> p (h d)"), ident[:])
                        last.then_inc(attT_done, 1)
                    scores(3)
                    weighted(3)
                    scoresT(2)
                    if s.has(-3):
                        pe.wait_ge(attT_copied, s.row(-2))
                        if s.has(1):
                            pe.wait_ge(v_copied, s.row(2))
                        elif s.has(-4):
                            pe.wait_ge(y_set, s.row(-3))
                        for t in range(QT):
                            last = nc.tensor.matmul(bank_v[:, t * D:(t + 1) * D], attT[:, t * P:(t + 1) * P], wp[:], start=True, stop=True)
                        last.then_inc(proj_done, 1)
                    if s.has(3):
                        pe.wait_ge(xn_set, s.row(4))
                        wait(pe, zT_copied, s.row(3))
                        wait(pe, attT_copied, s.row(-2))
                        for t in range(QT):
                            last = nc.tensor.transpose(bank_T[:, t * P:(t + 1) * P], xn[s.buf(3)][:, t, :], ident[:])
                        last.then_inc(zT_done, 1)
                    scoresT(3)

                all_slots(pe, slot)


def triangle_projections(nc, outgoing, x, ab, tokens, ln_w, ln_b, w_parts, b_parts):
    L, T, D = x.shape
    JT = T // P
    CB = ab.shape[4]
    NCB = ab.shape[2]
    GI = 2
    SI = 16
    G = L // GI
    GS = SI // GI
    TILES = GI * JT
    assert D == P and NCB * CB == 2 * D and TILES * P == 512

    x_v = x.rearrange("(s i) (t p) c -> s p t i c", i=SI, p=P) if outgoing else x.rearrange("(t p) (s i) c -> s p t i c", i=SI, p=P)
    ab_v = ab.rearrange("t p n (s i) c -> s t p n (i c)", i=SI)

    with ExitStack() as ctx:
        tag = "po_" if outgoing else "pi_"

        def sb(name, shape, dt=F32):
            return ctx.enter_context(nc.sbuf_tensor(tag + name, shape, dt))

        def bank(name):
            return ctx.enter_context(nc.psum_tensor(tag + name, [P, 512], F32))

        def sem(name):
            return ctx.enter_context(nc.semaphore(tag + name))

        NW = 4 * D
        ident, one_col, table_loaded = sb("ident", [P, P]), sb("one_col", [P, 1]), sb("table_loaded", [P, 1])
        half_neg, eps, zero = (sb(n, [P, JT, GI]) for n in ("half_neg", "eps", "zero"))
        g_col, b_col, b_wide, minus_mean = sb("g_col", [P, 1]), sb("b_col", [P, 1]), sb("b_wide", [P, P]), sb("minus_mean", [P, P])
        b_mean = sb("b_mean", [P, P])
        w_raw, w_gain, bias, w_part, w = (sb(n, [P, NW]) for n in ("w_raw", "w_gain", "bias", "w_part", "w"))
        w_hi, w_lo = sb("w_hi", [P, NW], F32R), sb("w_lo", [P, NW], F32R)
        x_in = [sb(f"x_in{i}", [P, JT, SI, D]) for i in range(2)]
        ab_out = [sb(f"ab_out{i}", [P, JT, NCB, SI, CB]) for i in range(2)]
        stats = [sb(f"stats{i}", [P, JT, GI, 6]) for i in range(2)]
        mean_var = [sb(f"mean_var{i}", [P, JT, GI, 2]) for i in range(2)]
        var_eps = [sb(f"var_eps{i}", [P, JT, GI]) for i in range(2)]
        mean_scaled = [sb(f"mean_scaled{i}", [P, JT, GI]) for i in range(2)]
        rstd_shift = [sb(f"rstd_shift{i}", [P, 2, JT, GI]) for i in range(2)]
        xn = [sb(f"xn{i}", [P, JT, GI, D]) for i in range(2)]
        zT_hi, zT_lo = ([sb(f"{n}{i}", [P, TILES, P], F32R) for i in range(2)] for n in ("zT_hi", "zT_lo"))
        sig = [sb(f"sig{i}", [P, 2 * D]) for i in range(TILES)]
        bank_T = [bank(f"bank_T{i}") for i in range(2)]
        bank_ab = [bank(f"bank_ab{i}") for i in range(4)]

        w_loaded, consts_set, w_gained, w_mm, w_set = (sem(n) for n in ("w_loaded", "consts_set", "w_gained", "w_mm", "w_set"))
        x_loaded, ab_stored = ([sem(f"{n}{i}") for i in range(2)] for n in ("x_loaded", "ab_stored"))
        stats_set, mean_set, eps_set, rstd_set, scaled_set, shift_set, xn_set, zT_done, hi_set, lo_set, ab_done, sig_set, ab_set, tokens_set = (sem(n) for n in (
            "stats_set", "mean_set", "eps_set", "rstd_set", "scaled_set", "shift_set", "xn_set", "zT_done", "hi_set", "lo_set", "ab_done", "sig_set", "ab_set", "tokens_set"))

        LOADS = L // SI

        class Slot:

            def __init__(self, it, s0):
                self.it, self.s0, self.loop = it, s0, not isinstance(it, int)

            def has(self, k):
                return self.loop or 0 <= self.s0 + k < G

            def group(self, k):
                return self.it * (2 * GS) + (self.s0 + k)

            def column(self, k):
                return self.it * (2 * GS * GI) + (self.s0 + k) * GI

            def turn(self, k):
                return self.it + (self.s0 + k) // (2 * GS)

            def buf(self, k):
                return (self.s0 + k) // GS % 2

            def pos(self, k):
                return (self.s0 + k) % GS

        def all_slots(slot, after_first=None):
            def run(engine):
                for s in range(-5, 0):
                    slot(Slot(0, s))
                    if s == -5 and after_first:
                        after_first()
                with engine.Fori(0, LOADS // 2 - 1) as it:
                    for s in range(2 * GS):
                        slot(Slot(it, s))
                for s in range(G - 2 * GS, G):
                    slot(Slot(0, s))
            return run

        AB_AHEAD, STORED_AHEAD = TILES, 1

        with nc.Block() as block:

            @block.sync
            def _(sp):
                def load(n, buf):
                    for t in range(JT):
                        for half in (slice(0, SI // 2), slice(SI // 2, SI)):
                            sp.dma_start(x_in[buf][:, t, half, :], x_v[n, :, t, half]).then_inc(x_loaded[buf], 16)

                def store(n, buf):
                    sp.wait_ge(ab_set, (n + 1) * (GS * TILES) + AB_AHEAD)
                    for t in range(JT):
                        sp.dma_start(ab_v[n, t], ab_out[buf][:, t, :, :, :].rearrange("p n i c -> p n (i c)")).then_inc(ab_stored[buf], 16)

                load(0, 0)
                sp.dma_start(g_col[:], ln_w.rearrange("(c a) -> c a", a=1)).then_inc(w_loaded, 16)
                sp.dma_start(b_col[:], ln_b.rearrange("(c a) -> c a", a=1)).then_inc(w_loaded, 16)
                for i in range(4):
                    sp.dma_start(w_raw[:, i * D:(i + 1) * D], w_parts[i]).then_inc(w_loaded, 16)
                    sp.dma_start(bias[:, i * D:(i + 1) * D], b_parts[i].rearrange("(a c) -> a c", a=1).to_broadcast([P, D])).then_inc(w_loaded, 16)
                load(1, 1)
                with sp.Fori(0, LOADS // 2 - 1) as it:
                    for buf in range(2):
                        sp.wait_ge(xn_set, (it * 2 + (buf + 1)) * GS)
                        load(it * 2 + (buf + 2), buf)
                        store(it * 2 + buf, buf)
                for buf in range(2):
                    store(LOADS - 2 + buf, buf)
                for buf in range(2):
                    sp.wait_ge(ab_stored[buf], LOADS // 2 * JT * 16 + STORED_AHEAD)

            @block.gpsimd
            def _(pool):
                nc.gpsimd.memset(minus_mean[:], -1.0 / D)
                nc.gpsimd.memset(one_col[:], 1.0)
                nc.gpsimd.memset(half_neg[:], -0.5)
                nc.gpsimd.memset(eps[:], EPS)
                nc.gpsimd.memset(zero[:], 0.0)
                nc.gpsimd.memset(ident[:], 0.0).then_inc(consts_set, 1)
                pool.wait_ge(consts_set, 1)
                nc.gpsimd.affine_select(out=ident[:], in_=ident[:], compare_op=ALU.not_equal, fill=1.0, base=0,
                                        pattern=[[-1, P]], channel_multiplier=1).then_inc(consts_set, 1)

                def slot(s):
                    if s.has(5):
                        b = s.pos(5) % 2
                        pool.wait_ge(mean_set, s.group(6))
                        nc.gpsimd.tensor_tensor(var_eps[b][:], mean_var[b][:, :, :, 1], eps[:], ALU.add).then_inc(eps_set, 1)
                        pool.wait_ge(eps_set, s.group(6))
                        if s.has(3):
                            pool.wait_ge(xn_set, s.group(4))
                        nc.gpsimd.tensor_tensor(rstd_shift[b][:, 0], var_eps[b][:], half_neg[:], ALU.pow).then_inc(rstd_set, 1)
                        pool.wait_ge(rstd_set, s.group(6))
                        nc.gpsimd.tensor_tensor(mean_scaled[b][:], mean_var[b][:, :, :, 0], rstd_shift[b][:, 0], ALU.mult).then_inc(scaled_set, 1)
                        pool.wait_ge(scaled_set, s.group(6))
                        nc.gpsimd.tensor_tensor(rstd_shift[b][:, 1], zero[:], mean_scaled[b][:], ALU.subtract).then_inc(shift_set, 1)

                all_slots(slot)(pool)

            @block.vector
            def _(dve):
                dve.sem_inc(ab_set, AB_AHEAD)
                for buf in range(2):
                    dve.sem_inc(ab_stored[buf], STORED_AHEAD)

                def slot(s):
                    def gated(tile):
                        dve.wait_ge(sig_set, s.group(0) * TILES + (tile + 1))
                        t, i = tile // GI, tile % GI
                        nc.vector.tensor_tensor(ab_out[s.buf(0)][:, t, :, s.pos(0) * GI + i, :],
                                                bank_ab[tile][:, 2 * D:4 * D].rearrange("p (n c) -> p n c", c=CB),
                                                sig[tile][:].rearrange("p (n c) -> p n c", c=CB), ALU.mult).then_inc(ab_set, 1)

                    if s.has(5):
                        b = s.pos(5) % 2
                        if s.pos(5) == 0:
                            dve.wait_ge(x_loaded[s.buf(5)], (s.turn(5) + 1) * (2 * 16 * JT))
                        for t in range(JT):
                            for i in range(GI):
                                last = nc.vector.bn_stats(stats[b][:, t, i, :], x_in[s.buf(5)][:, t, s.pos(5) * GI + i, :])
                        last.then_inc(stats_set, 1)
                    if s.has(1):
                        b = s.pos(1) % 2
                        dve.wait_ge(hi_set, s.group(2))
                        if s.has(-1):
                            dve.wait_ge(ab_done, s.group(0) * TILES)
                        nc.vector.scalar_tensor_tensor(out=zT_lo[b][:].rearrange("p a b -> p (a b)"), in0=bank_T[b][:], scalar=1.0,
                                                       in1=zT_hi[b][:].rearrange("p a b -> p (a b)").bitcast(F32), op0=ALU.add, op1=ALU.subtract).then_inc(lo_set, 1)
                    if s.has(0):
                        if s.pos(0) == 0:
                            dve.wait_ge(ab_stored[s.buf(0)], s.turn(0) * (16 * JT) + STORED_AHEAD)
                        gated(0)
                        gated(1)
                    if s.has(3):
                        dve.wait_ge(shift_set, s.group(4))
                        at = s.column(3)
                        columns = slice(at, at + GI) if isinstance(at, int) else bass.ds(at, GI)
                        nc.vector.tensor_copy(tokens[:, :, :, columns], rstd_shift[s.pos(3) % 2][:]).then_inc(tokens_set, 1)
                    if s.has(5):
                        dve.wait_ge(stats_set, s.group(6))
                    if s.has(0):
                        gated(2)
                    if s.has(5):
                        b = s.pos(5) % 2
                        for t in range(JT):
                            for i in range(GI):
                                last = nc.vector.bn_aggr(mean_var[b][:, t, i, :], stats[b][:, t, i, :])
                        last.then_inc(mean_set, 1)
                    if s.has(0):
                        gated(3)

                def prepare_weights():
                    dve.wait_ge(w_loaded, 10 * 16)
                    nc.vector.tensor_copy(b_wide[:], b_col[:, 0:1].to_broadcast([P, P])).then_inc(w_gained, 1)
                    nc.vector.tensor_scalar(w_gain[:], w_raw[:], g_col[:, 0:1], None, ALU.mult).then_inc(w_gained, 1)
                    dve.wait_ge(w_gained, 2)
                    nc.vector.tensor_scalar(b_mean[:], b_wide[:], 1.0 / D, None, ALU.mult).then_inc(w_gained, 1)
                    nc.vector.scalar_tensor_tensor(out=w_part[:], in0=bias[:], scalar=1.0 / D, in1=w_gain[:], op0=ALU.mult, op1=ALU.add).then_inc(w_gained, 1)
                    dve.wait_ge(w_gained, 4)
                    dve.wait_ge(w_mm, 1)
                    nc.vector.tensor_tensor(w[:], bank_ab[0][:], w_part[:], ALU.add).then_inc(w_set, 1)
                    dve.wait_ge(w_set, 1)
                    nc.vector.tensor_copy(w_hi[:], w[:]).then_inc(w_set, 1)
                    dve.wait_ge(w_set, 2)
                    nc.vector.tensor_tensor(w_lo[:], w[:], w_hi[:].bitcast(F32), ALU.subtract).then_inc(w_set, 1)

                all_slots(slot, prepare_weights)(dve)

            @block.scalar
            def _(act):
                act.wait_ge(consts_set, 1)
                nc.scalar.activation(table_loaded[:], one_col[:], ACT.Sigmoid)

                def slot(s):
                    def normalise(tile):
                        if s.has(3):
                            b, t, i = s.pos(3) % 2, tile // GI, tile % GI
                            if tile == 0:
                                act.wait_ge(shift_set, s.group(4))
                                if s.has(1):
                                    act.wait_ge(zT_done, s.group(2))
                            done = nc.scalar.activation(xn[b][:, t, i, :], x_in[s.buf(3)][:, t, s.pos(3) * GI + i, :], ACT.Identity,
                                                        bias=rstd_shift[b][:, 1, t, i:i + 1], scale=rstd_shift[b][:, 0, t, i:i + 1])
                            if tile == TILES - 1:
                                done.then_inc(xn_set, 1)

                    def sigmoid(tile):
                        if s.has(0):
                            act.wait_ge(ab_done, s.group(0) * TILES + (tile + 1))
                            nc.scalar.activation(sig[tile][:], bank_ab[tile][:, 0:2 * D], ACT.Sigmoid).then_inc(sig_set, 1)

                    if s.has(1):
                        b = s.pos(1) % 2
                        act.wait_ge(zT_done, s.group(2))
                        if s.has(-1):
                            act.wait_ge(ab_done, s.group(0) * TILES)
                        nc.scalar.activation(zT_hi[b][:].rearrange("p a b -> p (a b)"), bank_T[b][:], ACT.Identity, bias=one_col[:, 0:1]).then_inc(hi_set, 1)
                    for tile in range(TILES):
                        sigmoid(tile)
                        normalise(tile)

                all_slots(slot)(act)

            @block.tensor
            def _(pe):
                pe.wait_ge(consts_set, 2)
                pe.wait_ge(w_gained, 4)
                nc.tensor.matmul(bank_ab[0][:], minus_mean[:], w_gain[:], start=True, stop=False)
                nc.tensor.matmul(bank_ab[0][:], b_mean[:], w_raw[:], start=False, stop=True).then_inc(w_mm, 1)
                pe.wait_ge(w_set, 3)

                def slot(s):
                    if s.has(1):
                        b = s.pos(1) % 2
                        if s.has(-1):
                            pe.wait_ge(lo_set, s.group(0))
                        pe.wait_ge(xn_set, s.group(2))
                        for t in range(JT):
                            for i in range(GI):
                                last = nc.tensor.transpose(bank_T[b][:, (t * GI + i) * P:(t * GI + i + 1) * P], xn[b][:, t, i, :], ident[:])
                        last.then_inc(zT_done, 1)
                    if s.has(0):
                        b = s.pos(0) % 2
                        pe.wait_ge(lo_set, s.group(1))
                        for tile in range(TILES):
                            pe.wait_ge(ab_set, s.group(0) * TILES + (tile + 1 - TILES + AB_AHEAD))
                            nc.tensor.matmul(bank_ab[tile][:], zT_hi[b][:, tile, :], w_hi[:], start=True, stop=False)
                            nc.tensor.matmul(bank_ab[tile][:], zT_hi[b][:, tile, :], w_lo[:], start=False, stop=False)
                            nc.tensor.matmul(bank_ab[tile][:], zT_lo[b][:, tile, :], w_hi[:], start=False, stop=True).then_inc(ab_done, 1)

                all_slots(slot)(pe)


def triangle_product(nc, outgoing, x, x_out, ab, tokens, ln_w, ln_b, w_z, b_z, in_ln_w, in_ln_b, w_g, b_g):
    L, T, D = x.shape
    JT, _, NCB, _, CB = ab.shape
    NB = NCB // 2
    HALVES = L // P
    QUARTERS = HALVES * HALVES
    GK = 4
    EG = P // GK
    SLOTS = EG // NB * 2
    ITS = NB // 2
    BH = CB // 4
    assert SLOTS == 4 and BH == 2 and GK * P == 512

    ab_v = ab.rearrange("t p n i c -> n p t (i c)")
    x_v = x.rearrange("(h p) (f k) c -> h f p k c", p=P, k=GK)
    out_v = x_out.rearrange("(h p) (f k) c -> h f p k c", p=P, k=GK)

    with ExitStack() as ctx:
        tag = "to_" if outgoing else "ti_"

        def sb(name, shape, dt=F32):
            return ctx.enter_context(nc.sbuf_tensor(tag + name, shape, dt))

        def bank(name):
            return ctx.enter_context(nc.psum_tensor(tag + name, [P, 512], F32))

        def sem(name):
            return ctx.enter_context(nc.semaphore(tag + name))

        ident, one_col = sb("ident", [P, P]), sb("one_col", [P, 1])
        half_neg, eps = sb("half_neg", [P, GK]), sb("eps", [P, GK])
        g_col, b_col = sb("g_col", [P, 2]), sb("b_col", [P, 2])
        w = sb("w", [P, 2, D])
        a_in = [sb(f"a_in{i}", [P, JT, P, CB]) for i in range(2)]
        b_in = [sb(f"b_in{i}", [P, JT, P, CB]) for i in range(2)]
        p_acc = [sb(f"p_acc{i}", [P, P, D]) for i in range(2)]
        stats = [sb(f"stats{i}", [P, GK, 6]) for i in range(2)]
        mean_var = [sb(f"mean_var{i}", [P, GK, 2]) for i in range(2)]
        var_eps = [sb(f"var_eps{i}", [P, GK]) for i in range(2)]
        rstd = [sb(f"rstd{i}", [P, GK]) for i in range(2)]
        pn = [sb(f"pn{i}", [P, GK, D]) for i in range(2)]
        pT = [sb(f"pT{i}", [P, GK, P]) for i in range(2)]
        x_in = [sb(f"x_in{i}", [P, GK, D]) for i in range(SLOTS)]
        xn = [sb(f"xn{i}", [P, GK, D]) for i in range(2)]
        xT = [sb(f"xT{i}", [P, GK, P]) for i in range(2)]
        gate = [sb(f"gate{i}", [P, GK, D]) for i in range(2)]
        y = [sb(f"y{i}", [P, GK, D]) for i in range(2)]
        w_raw, w_gain, bias, w_part, b_wide, b_mean = (p_acc[1][:, 2 * i:2 * i + 2, :] for i in range(6))
        minus_mean = p_acc[1][:, 12, :]
        bank_p = [bank(f"bank_p{i}") for i in range(2)]
        bank_T, bank_X = bank("bank_T"), bank("bank_X")
        bank_z = [bank(f"bank_z{i}") for i in range(2)]
        bank_g = [bank(f"bank_g{i}") for i in range(2)]

        w_loaded, consts_set, w_gained, w_mm, w_set = (sem(n) for n in ("w_loaded", "consts_set", "w_gained", "w_mm", "w_set"))
        ab_loaded, y_stored = ([sem(f"{n}{i}") for i in range(2)] for n in ("ab_loaded", "y_stored"))
        x_loaded = [sem(f"x_loaded{i}") for i in range(SLOTS)]
        p_done, p_copied, stats_set, mean_set, eps_set, rstd_set, pn_set, xn_set, pT_done, xT_done, pT_copied, xT_copied, z_done, g_done, gate_set, gated_set, y_set = (
            sem(n) for n in ("p_done", "p_copied", "stats_set", "mean_set", "eps_set", "rstd_set", "pn_set", "xn_set", "pT_done", "xT_done", "pT_copied",
                             "xT_copied", "z_done", "g_done", "gate_set", "gated_set", "y_set"))
        tokens_turned, tokens_set, xn_scaled = sem("tokens_turned"), sem("tokens_set"), sem("xn_scaled")

        P_AHEAD, GATE_AHEAD, GATED_AHEAD, Z_AHEAD, G_AHEAD, Y_AHEAD, STORED_AHEAD = 2, 2, 2, 1, 1, 2, 1

        class Slot:

            def __init__(self, quarter, it, j):
                self.quarter, self.it, self.j = quarter, it, j
                self.last = isinstance(it, int) and it == ITS - 1

            def group(self, k):
                return self.it * SLOTS + ((self.quarter - 1) * EG + self.j + k)

            def has(self, k):
                return not (self.quarter == QUARTERS and self.last and self.j + k >= SLOTS)

            def place(self, k):
                if self.last and self.j + k >= SLOTS:
                    return self.quarter, (self.j + k - SLOTS) * GK
                return self.quarter - 1, self.it * (SLOTS * GK) + (self.j + k) * GK

            def x_uses(self, k):
                return self.it + ((self.quarter - 1) * ITS + (self.j + k) // SLOTS + 1)

        def banks_of(it, j):
            if isinstance(it, int):
                return range(2 * j, 2 * j + 2) if j < SLOTS // 2 else ()
            return (j,)

        def steps(engine, slot, first):
            for quarter in range(first, QUARTERS + 1):
                with engine.Fori(0, ITS - 1) as it:
                    for j in range(SLOTS):
                        slot(quarter, it, j)
                for j in range(SLOTS):
                    slot(quarter, ITS - 1, j)
                yield quarter

        def act_share(quarter):
            return 3 if quarter == QUARTERS else 2

        def of_token(v, place, k):
            quarter, at = place[0], place[1] + (place[0] % HALVES * P + k)
            row = tokens[:, v, quarter // HALVES]
            return row[:, at:at + 1] if isinstance(at, int) else row[:, bass.ds(at, 1)]

        with nc.Block() as block:

            @block.sync
            def _(sp):
                def load_ab(quarter, block_at, buf):
                    ih, kh = quarter // HALVES, quarter % HALVES
                    n = P * CB
                    sp.dma_start(a_in[buf][:].rearrange("p t i c -> p t (i c)"), ab_v[block_at, :, :, ih * n:(ih + 1) * n]).then_inc(ab_loaded[buf], 16)
                    sp.dma_start(b_in[buf][:].rearrange("p t i c -> p t (i c)"), ab_v[block_at + NB, :, :, kh * n:(kh + 1) * n]).then_inc(ab_loaded[buf], 16)

                def load_x(quarter, group, buf):
                    ih, kh = quarter // HALVES, quarter % HALVES
                    sp.dma_start(x_in[buf][:], x_v[ih, group + kh * EG]).then_inc(x_loaded[buf], 16)

                load_ab(0, 0, 0)
                for i, (gain, offset, weight, add) in enumerate(((ln_w, ln_b, w_z, b_z), (in_ln_w, in_ln_b, w_g, b_g))):
                    sp.dma_start(g_col[:, i:i + 1], gain.rearrange("(c a) -> c a", a=1)).then_inc(w_loaded, 16)
                    sp.dma_start(b_col[:, i:i + 1], offset.rearrange("(c a) -> c a", a=1)).then_inc(w_loaded, 16)
                    sp.dma_start(w_raw[:, i, :], weight).then_inc(w_loaded, 16)
                    sp.dma_start(bias[:, i, :], add.rearrange("(a c) -> a c", a=1).to_broadcast([P, D])).then_inc(w_loaded, 16)
                load_ab(0, 1, 1)
                for buf in range(SLOTS):
                    load_x(0, buf, buf)

                def slot(quarter, it, j):
                    last = isinstance(it, int)
                    if j % 2 == 0 and quarter < QUARTERS and not (last and quarter == QUARTERS - 1):
                        buf = j // 2
                        sp.wait_ge(p_done, it * (2 * BH) + (quarter * NB + buf + 1) * BH)
                        if last:
                            load_ab(quarter + 1, buf, buf)
                        else:
                            load_ab(quarter, it * 2 + (buf + 2), buf)
                    if quarter > 0:
                        sp.wait_ge(y_set, it * SLOTS + ((quarter - 1) * EG + j + 1 + Y_AHEAD))
                        ih, kh = (quarter - 1) // HALVES, (quarter - 1) % HALVES
                        sp.dma_start(out_v[ih, it * SLOTS + (kh * EG + j)], y[j % 2][:]).then_inc(y_stored[j % 2], 16)
                        if not last:
                            load_x(quarter - 1, it * SLOTS + (j + SLOTS), j)
                        elif quarter < QUARTERS:
                            load_x(quarter, j, j)

                for _ in steps(sp, slot, 0):
                    pass
                for buf in range(2):
                    sp.wait_ge(y_stored[buf], QUARTERS * EG // 2 * 16 + STORED_AHEAD)

            @block.gpsimd
            def _(pool):
                pool.sem_inc(y_set, Y_AHEAD)
                for buf in range(2):
                    pool.sem_inc(y_stored[buf], STORED_AHEAD)
                nc.gpsimd.memset(minus_mean, -1.0 / D)
                nc.gpsimd.memset(one_col[:], 1.0)
                nc.gpsimd.memset(half_neg[:], -0.5)
                nc.gpsimd.memset(eps[:], EPS)
                nc.gpsimd.memset(ident[:], 0.0).then_inc(consts_set, 1)
                pool.wait_ge(consts_set, 1)
                nc.gpsimd.affine_select(out=ident[:], in_=ident[:], compare_op=ALU.not_equal, fill=1.0, base=0,
                                        pattern=[[-1, P]], channel_multiplier=1).then_inc(consts_set, 1)

                def power(b, count):
                    pool.wait_ge(mean_set, count)
                    nc.gpsimd.tensor_tensor(var_eps[b][:], mean_var[b][:, :, 1], eps[:], ALU.add).then_inc(eps_set, 1)
                    pool.wait_ge(eps_set, count)
                    nc.gpsimd.tensor_tensor(rstd[b][:], var_eps[b][:], half_neg[:], ALU.pow).then_inc(rstd_set, 1)

                for e in range(3):
                    power(e % 2, e + 1)

                def slot(quarter, it, j):
                    s = Slot(quarter, it, j)
                    if s.has(3):
                        power(1 - j % 2, s.group(4))
                    b = j % 2
                    pool.wait_ge(y_stored[b], (it * (SLOTS // 2) + ((quarter - 1) * (EG // 2) + j // 2)) * 16 + STORED_AHEAD)
                    pool.wait_ge(gated_set, s.group(1) + GATED_AHEAD)
                    nc.gpsimd.tensor_tensor(y[b][:], gate[b][:], x_in[j][:], ALU.add).then_inc(y_set, 1)

                for _ in steps(pool, slot, 1):
                    pass

            @block.vector
            def _(dve):
                dve.sem_inc(gated_set, GATED_AHEAD)
                dve.wait_ge(w_loaded, 8 * 16)
                for i in range(2):
                    nc.vector.tensor_copy(b_wide[:, i, :], b_col[:, i:i + 1].to_broadcast([P, P]))
                    last = nc.vector.tensor_scalar(w_gain[:, i, :], w_raw[:, i, :], g_col[:, i:i + 1], None, ALU.mult)
                last.then_inc(w_gained, 1)
                dve.wait_ge(w_gained, 1)
                nc.vector.tensor_scalar(b_mean, b_wide, 1.0 / D, None, ALU.mult)
                nc.vector.scalar_tensor_tensor(out=w_part, in0=bias, scalar=1.0 / D, in1=w_gain, op0=ALU.mult, op1=ALU.add).then_inc(w_gained, 1)
                dve.wait_ge(w_gained, 2)
                dve.wait_ge(w_mm, 1)
                nc.vector.tensor_tensor(w[:], bank_z[0][:, 0:2 * D].rearrange("p (i c) -> p i c", i=2), w_part, ALU.add).then_inc(w_set, 1)
                if outgoing:
                    dve.wait_ge(tokens_turned, 1)
                    for v in range(2):
                        last = nc.vector.tensor_copy(tokens[:, v], bank_g[v][:].rearrange("p (h k) -> p h k", h=HALVES))
                    last.then_inc(tokens_set, 1)
                    dve.wait_ge(tokens_set, 1)

                def column(place, k):
                    quarter, col = place[0], place[1] + k
                    m = p_acc[quarter % 2]
                    return m[:, col, :] if isinstance(col, int) else m[:, bass.ds(col, 1), :].rearrange("p a c -> p (a c)")

                def statistics(b, place):
                    for k in range(GK):
                        last = nc.vector.bn_stats(stats[b][:, k, :], column(place, k))
                    last.then_inc(stats_set, 1)

                def aggregate(b):
                    for k in range(GK):
                        last = nc.vector.bn_aggr(mean_var[b][:, k, :], stats[b][:, k, :])
                    last.then_inc(mean_set, 1)

                def normalise(b, place, count):
                    dve.wait_ge(rstd_set, count)
                    for k in range(GK):
                        last = nc.vector.tensor_scalar(pn[b][:, k, :], column(place, k), mean_var[b][:, k, 0:1], rstd[b][:, k:k + 1],
                                                       ALU.subtract, ALU.mult)
                    last.then_inc(pn_set, 1)

                def normalise_x(b, buf, place, share):
                    for k in range(share, GK):
                        last = nc.vector.tensor_scalar(xn[b][:, k, :], x_in[buf][:, k, :], of_token(0, place, k), of_token(1, place, k), ALU.mult, ALU.add)
                    last.then_inc(xn_set, 1)

                dve.wait_ge(p_copied, NB * BH + P_AHEAD)
                for e in range(3):
                    statistics(e % 2, (0, e * GK))
                    dve.wait_ge(stats_set, e + 1)
                    if e == 2:
                        normalise(0, (0, 0), 1)
                        dve.wait_ge(pn_set, 1)
                    aggregate(e % 2)
                dve.wait_ge(x_loaded[0], 16)
                normalise_x(0, 0, (0, 0), act_share(0))

                def slot(quarter, it, j):
                    s = Slot(quarter, it, j)
                    b = j % 2
                    if s.has(1):
                        dve.wait_ge(pT_done, s.group(1))
                        normalise(1 - b, s.place(1), s.group(2))
                    if s.has(3):
                        if s.last and j + 3 == SLOTS:
                            dve.wait_ge(p_copied, (quarter + 1) * NB * BH + P_AHEAD)
                        statistics(1 - b, s.place(3))
                        dve.wait_ge(stats_set, s.group(4))
                    if s.has(1):
                        buf = (j + 1) % SLOTS
                        dve.wait_ge(x_loaded[buf], s.x_uses(1) * 16)
                        dve.wait_ge(xT_done, s.group(1))
                        normalise_x(1 - b, buf, s.place(1), act_share(quarter))
                    if s.has(3):
                        aggregate(1 - b)
                    dve.wait_ge(z_done, s.group(1) + Z_AHEAD)
                    dve.wait_ge(gate_set, s.group(1) + GATE_AHEAD)
                    flat = gate[b][:].rearrange("p k c -> p (k c)")
                    nc.vector.tensor_tensor(flat, bank_z[b][:], flat, ALU.mult).then_inc(gated_set, 1)

                for _ in steps(dve, slot, 1):
                    pass

            @block.scalar
            def _(act):
                act.sem_inc(p_copied, P_AHEAD)
                act.sem_inc(gate_set, GATE_AHEAD)
                act.wait_ge(consts_set, 1)

                def gather(quarter, it, j):
                    n = it * (2 * BH) + (quarter * NB * BH + j)
                    act.wait_ge(p_done, n + 1)
                    c0 = (j // BH) * CB + (j % BH) * 4 + it * (2 * CB)
                    cols = slice(c0, c0 + 4) if isinstance(c0, int) else bass.ds(c0, 4)
                    nc.scalar.activation(p_acc[quarter % 2][:, :, cols].rearrange("p k c -> p c k"), bank_p[j % 2][:].rearrange("p (c k) -> p c k", c=4),
                                         ACT.Identity).then_inc(p_copied, 1)

                def copy(b, count):
                    act.wait_ge(pT_done, count)
                    nc.scalar.activation(pT[b][:].rearrange("p a b -> p (a b)"), bank_T[:], ACT.Identity, bias=one_col[:, 0:1]).then_inc(pT_copied, 1)
                    act.wait_ge(xT_done, count)
                    nc.scalar.activation(xT[b][:].rearrange("p a b -> p (a b)"), bank_X[:], ACT.Identity, bias=one_col[:, 0:1]).then_inc(xT_copied, 1)

                def normalise_x(b, buf, place, share):
                    for k in range(share):
                        last = nc.scalar.activation(xn[b][:, k, :], x_in[buf][:, k, :], ACT.Identity, bias=of_token(1, place, k), scale=of_token(0, place, k))
                    last.then_inc(xn_scaled, 1)

                def slot(quarter, it, j):
                    if quarter < QUARTERS:
                        for j_bank in banks_of(it, j):
                            gather(quarter, it, j_bank)
                    if quarter > 0:
                        s = Slot(quarter, it, j)
                        b = j % 2
                        if s.has(1):
                            buf = (j + 1) % SLOTS
                            act.wait_ge(x_loaded[buf], s.x_uses(1) * 16)
                            normalise_x(1 - b, buf, s.place(1), act_share(quarter))
                        act.wait_ge(g_done, s.group(1) + G_AHEAD)
                        act.wait_ge(y_set, s.group(-1) + Y_AHEAD)
                        nc.scalar.activation(gate[b][:].rearrange("p k c -> p (k c)"), bank_g[b][:], ACT.Sigmoid).then_inc(gate_set, 1)
                        if s.has(1):
                            copy(1 - b, s.group(2))

                for quarter in steps(act, slot, 0):
                    if quarter == 0:
                        if outgoing:
                            act.wait_ge(tokens_set, 1)
                        act.wait_ge(x_loaded[0], 16)
                        normalise_x(0, 0, (0, 0), act_share(0))
                        copy(0, 1)

            @block.tensor
            def _(pe):
                pe.sem_inc(z_done, Z_AHEAD)
                pe.sem_inc(g_done, G_AHEAD)
                pe.wait_ge(consts_set, 2)
                if outgoing:
                    for v in range(2):
                        for ih in range(HALVES):
                            for t in range(JT):
                                last = nc.tensor.transpose(bank_g[v][:, (ih * JT + t) * P:(ih * JT + t + 1) * P], tokens[:, v, t, ih * P:(ih + 1) * P], ident[:])
                    last.then_inc(tokens_turned, 1)
                pe.wait_ge(w_gained, 2)
                nc.tensor.matmul(bank_z[0][:, 0:2 * D], minus_mean, w_gain.rearrange("p i c -> p (i c)"), start=True, stop=False)
                for i in range(2):
                    last = nc.tensor.matmul(bank_z[0][:, i * D:(i + 1) * D], b_mean[:, i, :], w_raw[:, i, :], start=False, stop=(i == 1))
                last.then_inc(w_mm, 1)
                pe.wait_ge(w_set, 1)

                def products(quarter, it, j):
                    buf, half = j // BH, j % BH
                    if half == 0:
                        pe.wait_ge(ab_loaded[buf], (it + (quarter * ITS + 1)) * 32)
                    pe.wait_ge(p_copied, it * (2 * BH) + (quarter * NB * BH + j + 1 - 2 + P_AHEAD))
                    for c in range(4):
                        for t in range(JT):
                            last = nc.tensor.matmul(bank_p[j % 2][:, c * P:(c + 1) * P], a_in[buf][:, t, :, half * 4 + c], b_in[buf][:, t, :, half * 4 + c],
                                                    start=(t == 0), stop=(t == JT - 1))
                    last.then_inc(p_done, 1)

                def turn(b, count):
                    for normal, bank_, normal_set, turned in ((pn[b], bank_T, pn_set, pT_done), (xn[b], bank_X, xn_set, xT_done)):
                        pe.wait_ge(normal_set, count)
                        if turned is xT_done:
                            pe.wait_ge(xn_scaled, count)
                        for k in range(GK):
                            last = nc.tensor.transpose(bank_[:, k * P:(k + 1) * P], normal[:, k, :], ident[:])
                        last.then_inc(turned, 1)

                def slot(quarter, it, j):
                    if quarter < QUARTERS:
                        for j_bank in banks_of(it, j):
                            products(quarter, it, j_bank)
                    if quarter > 0:
                        s = Slot(quarter, it, j)
                        b = j % 2
                        pe.wait_ge(pT_copied, s.group(1))
                        pe.wait_ge(gated_set, s.group(-1) + GATED_AHEAD)
                        for k in range(GK):
                            last = nc.tensor.matmul(bank_z[b][:, k * D:(k + 1) * D], pT[b][:, k, :], w[:, 0], start=True, stop=True)
                        last.then_inc(z_done, 1)
                        pe.wait_ge(xT_copied, s.group(1))
                        pe.wait_ge(gate_set, s.group(-1) + GATE_AHEAD)
                        for k in range(GK):
                            last = nc.tensor.matmul(bank_g[b][:, k * D:(k + 1) * D], xT[b][:, k, :], w[:, 1], start=True, stop=True)
                        last.then_inc(g_done, 1)
                        if s.has(1):
                            turn(1 - b, s.group(2))

                for quarter in steps(pe, slot, 0):
                    if quarter == 0:
                        turn(0, 1)


def pair_stack(nc, out, x, at_ln_g, at_ln_b, w_qkv, b_qkv, w_proj, b_proj, ln_in_w, ln_in_b, w_ag, b_ag, w_ap, b_ap,
               w_bg, b_bg, w_bp, b_bp, ln_out_w, ln_out_b, w_z, b_z, w_g, b_g):
    x, out = x[0], out[0]
    L, _, D = x.shape
    CB = 8
    x_at = nc.dram_tensor("x_at", (L, L, D), F32, kind="Internal").ap()
    x_mid = nc.dram_tensor("x_mid", (L, L, D), F32, kind="Internal").ap()
    ab = nc.dram_tensor("ab", (L // P, P, 2 * D // CB, L, CB), F32, kind="Internal").ap()

    attention_layer(nc, x, x_at, at_ln_g, at_ln_b, w_qkv, b_qkv, w_proj, b_proj)
    for idx, (outgoing, src, dst) in enumerate(((True, x_at, x_mid), (False, x_mid, out))):
        with nc.sbuf_tensor(f"tokens{idx}", [P, 2, L // P, L], F32) as tokens:
            nc.all_engine_barrier()
            triangle_projections(nc, outgoing, src, ab, tokens, ln_in_w[idx], ln_in_b[idx],
                                 [m[idx] for m in (w_ag, w_bg, w_ap, w_bp)], [m[idx] for m in (b_ag, b_bg, b_ap, b_bp)])
            nc.all_engine_barrier()
            triangle_product(nc, outgoing, src, dst, ab, tokens, ln_out_w[idx], ln_out_b[idx], w_z[idx], b_z[idx],
                             ln_in_w[idx], ln_in_b[idx], w_g[idx], b_g[idx])


_INS = ["x", "L0_conv_ln_g", "L0_conv_ln_b", "L0_conv_w_qkv", "L0_conv_b_qkv", "L0_conv_w_proj", "L0_conv_b_proj",
        "L1_conv_ln_in_w", "L1_conv_ln_in_b", "L1_conv_w_ag", "L1_conv_b_ag", "L1_conv_w_ap", "L1_conv_b_ap",
        "L1_conv_w_bg", "L1_conv_b_bg", "L1_conv_w_bp", "L1_conv_b_bp", "L1_conv_ln_out_w", "L1_conv_ln_out_b",
        "L1_conv_w_z", "L1_conv_b_z", "L1_conv_w_g", "L1_conv_b_g"]


def kernel(**inputs):
    import numpy as np
    import concourse.bacc as bacc
    from concourse.bass_utils import run_bass_kernel_spmd

    nc = bacc.Bacc("TRN2", target_bir_lowering=False, num_devices=1)
    arrays = {f"in_{name}": np.ascontiguousarray(inputs[name]) for name in _INS}
    ins = [nc.dram_tensor(name, a.shape, mybir.dt.from_np(a.dtype), kind="ExternalInput").ap() for name, a in arrays.items()]
    out = nc.dram_tensor("out", arrays["in_x"].shape, F32, kind="ExternalOutput").ap()
    pair_stack(nc, out, *ins)
    return run_bass_kernel_spmd(nc, [arrays], core_ids=[0]).results[0]["out"]
```
